# Optimizing a Trainium2 kernel written in Bass

```python
import numpy as np
import jax
import jax.numpy as jnp

def _softmax(x, axis=-1):
    return jax.nn.softmax(x, axis=axis)

def _gelu(x):
    return jax.nn.gelu(x, approximate=True)

def _silu(x):
    return jax.nn.silu(x)

def _sigmoid(x):
    return jax.nn.sigmoid(x)

def _layernorm(x, axis=-1, eps=1e-05):
    m = jnp.mean(x, axis=axis, keepdims=True)
    v = jnp.var(x, axis=axis, keepdims=True)
    return (x - m) / jnp.sqrt(v + eps)

def _scatter_add(tgt, idx, src, axis=0):
    return tgt.at[idx].add(src)

def _segment_sum(src, seg, n):
    return jax.ops.segment_sum(src, seg, n)
kernel_name = 'mk_gnn_resnorm_d2_gnn_r8_17d0fb'

def setup_inputs(seed: int=0):
    np.random.seed(seed)
    _w = jnp.asarray

    def _rec_inputs():
        import jax
        import jax.numpy as jnp
        _gk = jax.random.key(seed)
        x = -0.0003713 + 1 * jax.random.normal(jax.random.fold_in(_gk, 1), (12500, 128), jnp.float32)
        src = jax.random.randint(jax.random.fold_in(_gk, 2), (400000,), 0, 12500, jnp.int32)
        dst = jnp.minimum((12500 * jax.random.uniform(jax.random.fold_in(_gk, 3), (400000,)) ** 2.0).astype(jnp.int32), 99999)
        _o = jnp.argsort(dst, stable=True)
        src = src[_o]
        dst = dst[_o]
        edge_attr_64 = 0.000102155 + 1.00015 * jax.random.normal(jax.random.fold_in(_gk, 12), (400000, 64), jnp.float32)
        edge_weight = jax.random.uniform(jax.random.fold_in(_gk, 14), (400000,), jnp.float32, 0.0, 0.999999)
        return (x, src, dst, edge_attr_64, edge_weight)
    x, src, dst, edge_attr_64, edge_weight = _rec_inputs()

    def _L0_gnn_setup():
        import jax, jax.numpy as jnp
        import numpy as np
        N_NODES = 12500
        N_EDGES = 200000
        IN_FEATS = 128
        HIDDEN = 150
        NUM_OUT = 128

        def _mean_agg(h, src, dst, deg_inv):
            summed = jax.ops.segment_sum(h[src], dst, num_segments=N_NODES)
            return summed * deg_inv[:, None]

        def _sage_conv(h, src, dst, deg_inv, W_self, W_neigh, b):
            h_neigh = _mean_agg(h, src, dst, deg_inv)
            return h @ W_self + h_neigh @ W_neigh + b
        key = jax.random.key(seed)
        ks = jax.random.split(key, 9)
        x = jax.random.normal(ks[0], (N_NODES, IN_FEATS), dtype=jnp.float32)
        src = jax.random.randint(ks[1], (N_EDGES,), 0, N_NODES, dtype=jnp.int32)
        dst = jax.random.randint(ks[2], (N_EDGES,), 0, N_NODES, dtype=jnp.int32)

        def lin(k, fan_in, fan_out):
            bound = 1.0 / np.sqrt(fan_in)
            return jax.random.uniform(k, (fan_in, fan_out), jnp.float32, -bound, bound)
        W_self1 = lin(ks[3], IN_FEATS, HIDDEN)
        W_neigh1 = lin(ks[4], IN_FEATS, HIDDEN)
        b1 = jnp.zeros((HIDDEN,), jnp.float32)
        W_self2 = lin(ks[5], HIDDEN, NUM_OUT)
        W_neigh2 = lin(ks[6], HIDDEN, NUM_OUT)
        b2 = jnp.zeros((NUM_OUT,), jnp.float32)
        return {'x': x, 'src': src, 'dst': dst, 'W_self1': W_self1, 'W_neigh1': W_neigh1, 'b1': b1, 'W_self2': W_self2, 'W_neigh2': W_neigh2, 'b2': b2}
    _L0_gnn_all = _L0_gnn_setup()
    _L0_gnn_in = {k: v for k, v in _L0_gnn_all.items() if k in ('W_self1', 'W_neigh1', 'b1', 'W_self2', 'W_neigh2', 'b2')}
    del _L0_gnn_all

    def _L1_gnn_setup():
        import jax, jax.numpy as jnp
        import numpy as np
        N_NODES = 12500
        N_EDGES = 62500
        IN_CH = 128
        EDGE_CH = 64

        def _glorot(key, shape):
            fan_in, fan_out = (shape[0], shape[1])
            lim = (6.0 / (fan_in + fan_out)) ** 0.5
            return jax.random.uniform(key, shape, jnp.float32, -lim, lim)
        key = jax.random.key(seed)
        ks = jax.random.split(key, 14)
        x = jax.random.normal(ks[0], (N_NODES, IN_CH), jnp.float32)
        edge_index = jax.random.randint(ks[1], (2, N_EDGES), 0, N_NODES, jnp.int64)
        edge_attr = jax.random.normal(ks[2], (N_EDGES, EDGE_CH), jnp.float32)
        timestamps = jax.random.uniform(ks[3], (N_EDGES,), jnp.float32)
        We1 = _glorot(ks[4], (EDGE_CH, 2 * EDGE_CH))
        be1 = jnp.zeros((2 * EDGE_CH,), jnp.float32)
        We2 = _glorot(ks[5], (2 * EDGE_CH, IN_CH))
        be2 = jnp.zeros((IN_CH,), jnp.float32)
        Wt = _glorot(ks[6], (1, IN_CH))
        bt = jnp.zeros((IN_CH,), jnp.float32)
        Wn1 = _glorot(ks[7], (2 * IN_CH, IN_CH))
        bn1 = jnp.zeros((IN_CH,), jnp.float32)
        Wn2 = _glorot(ks[8], (IN_CH, IN_CH))
        bn2 = jnp.zeros((IN_CH,), jnp.float32)
        return {'x': x, 'edge_index': edge_index, 'edge_attr': edge_attr, 'timestamps': timestamps, 'We1': We1, 'be1': be1, 'We2': We2, 'be2': be2, 'Wt': Wt, 'bt': bt, 'Wn1': Wn1, 'bn1': bn1, 'Wn2': Wn2, 'bn2': bn2}
    _L1_gnn_all = _L1_gnn_setup()
    _L1_gnn_in = {k: v for k, v in _L1_gnn_all.items() if k in ('We1', 'be1', 'We2', 'be2', 'Wt', 'bt', 'Wn1', 'bn1', 'Wn2', 'bn2')}
    del _L1_gnn_all
    return {'x': x, 'src': src, 'dst': dst, 'edge_attr_64': edge_attr_64, 'edge_weight': edge_weight, 'L0_gnn_W_self1': _L0_gnn_in['W_self1'], 'L0_gnn_W_neigh1': _L0_gnn_in['W_neigh1'], 'L0_gnn_b1': _L0_gnn_in['b1'], 'L0_gnn_W_self2': _L0_gnn_in['W_self2'], 'L0_gnn_W_neigh2': _L0_gnn_in['W_neigh2'], 'L0_gnn_b2': _L0_gnn_in['b2'], 'L1_gnn_We1': _L1_gnn_in['We1'], 'L1_gnn_be1': _L1_gnn_in['be1'], 'L1_gnn_We2': _L1_gnn_in['We2'], 'L1_gnn_be2': _L1_gnn_in['be2'], 'L1_gnn_Wt': _L1_gnn_in['Wt'], 'L1_gnn_bt': _L1_gnn_in['bt'], 'L1_gnn_Wn1': _L1_gnn_in['Wn1'], 'L1_gnn_bn1': _L1_gnn_in['bn1'], 'L1_gnn_Wn2': _L1_gnn_in['Wn2'], 'L1_gnn_bn2': _L1_gnn_in['bn2']}

def reference(x, src, dst, edge_attr_64, edge_weight, L0_gnn_W_self1, L0_gnn_W_neigh1, L0_gnn_b1, L0_gnn_W_self2, L0_gnn_W_neigh2, L0_gnn_b2, L1_gnn_We1, L1_gnn_be1, L1_gnn_We2, L1_gnn_be2, L1_gnn_Wt, L1_gnn_bt, L1_gnn_Wn1, L1_gnn_bn1, L1_gnn_Wn2, L1_gnn_bn2):
    import jax
    import jax.numpy as jnp

    def _L0_gnn_ref(x, src, dst, W_self1, W_neigh1, b1, W_self2, W_neigh2, b2):
        import jax, jax.numpy as jnp
        import numpy as np
        N_NODES = 12500
        N_EDGES = 200000
        IN_FEATS = 128
        HIDDEN = 150
        NUM_OUT = 128

        def _mean_agg(h, src, dst, deg_inv):
            summed = jax.ops.segment_sum(h[src], dst, num_segments=N_NODES)
            return summed * deg_inv[:, None]

        def _sage_conv(h, src, dst, deg_inv, W_self, W_neigh, b):
            h_neigh = _mean_agg(h, src, dst, deg_inv)
            return h @ W_self + h_neigh @ W_neigh + b
        deg = jax.ops.segment_sum(jnp.ones((src.shape[0],), x.dtype), dst, num_segments=N_NODES)
        deg_inv = jnp.where(deg > 0, 1.0 / jnp.maximum(deg, 1.0), 0.0)
        h = _sage_conv(x, src, dst, deg_inv, W_self1, W_neigh1, b1)
        h = jax.nn.relu(h)
        h = _sage_conv(h, src, dst, deg_inv, W_self2, W_neigh2, b2)
        return h

    def _L1_gnn_ref(x, edge_index, edge_attr, timestamps, We1, be1, We2, be2, Wt, bt, Wn1, bn1, Wn2, bn2):
        import jax, jax.numpy as jnp
        import numpy as np
        N_NODES = 12500
        N_EDGES = 62500
        IN_CH = 128
        EDGE_CH = 64

        def _glorot(key, shape):
            fan_in, fan_out = (shape[0], shape[1])
            lim = (6.0 / (fan_in + fan_out)) ** 0.5
            return jax.random.uniform(key, shape, jnp.float32, -lim, lim)
        ts = timestamps[:, None]
        ef = jax.nn.relu(edge_attr @ We1 + be1) @ We2 + be2
        tw = jax.nn.sigmoid(ts @ Wt + bt)
        ef = ef * tw
        row, col = (edge_index[0], edge_index[1])
        combined = jnp.concatenate([x[row], ef], axis=1)
        msg = jax.nn.relu(combined @ Wn1 + bn1) @ Wn2 + bn2
        out = jax.ops.segment_sum(msg, col, num_segments=x.shape[0])
        return out + x
    edge_index = jnp.stack([src, dst])
    x = _layernorm(x + _L0_gnn_ref(x, src, dst, L0_gnn_W_self1, L0_gnn_W_neigh1, L0_gnn_b1, L0_gnn_W_self2, L0_gnn_W_neigh2, L0_gnn_b2), axis=-1)
    x = _layernorm(x + _L1_gnn_ref(x, edge_index, edge_attr_64, edge_weight, L1_gnn_We1, L1_gnn_be1, L1_gnn_We2, L1_gnn_be2, L1_gnn_Wt, L1_gnn_bt, L1_gnn_Wn1, L1_gnn_bn1, L1_gnn_Wn2, L1_gnn_bn2), axis=-1)
    return x

_drawn_inputs = setup_inputs


def setup_inputs(seed=0):
    import zlib

    import numpy as np

    out = dict(_drawn_inputs(seed))
    spreads = {'L0_gnn_b1': (0.0, 0.1),
     'L0_gnn_b2': (0.0, 0.1),
     'L1_gnn_be1': (0.0, 0.377),
     'L1_gnn_be2': (0.0, 0.1),
     'L1_gnn_bt': (0.0, 0.748),
     'L1_gnn_bn1': (0.0, 0.1),
     'L1_gnn_bn2': (0.0, 0.1)}
    factors = {'edge_weight': 8.0, 'L0_gnn_W_neigh1': 2.978, 'L1_gnn_Wt': 8.0}
    for name, (base, spread) in spreads.items():
        noise = np.random.default_rng([zlib.crc32(name.encode()), seed]).standard_normal(out[name].shape)
        drawn = base * np.exp(spread * noise) if base else spread * noise
        out[name] = jnp.asarray(drawn.astype(out[name].dtype))
    for name, factor in factors.items():
        out[name] = (out[name] * factor).astype(out[name].dtype)
    return out
```

```python
from contextlib import ExitStack

import concourse.bass as bass
from concourse import mybir

FP32 = mybir.dt.float32
BF16 = mybir.dt.bfloat16
I32 = mybir.dt.int32
ALU = mybir.AluOpType
ACT = mybir.ActivationFunctionType
AX = mybir.AxisListType
ds = bass.ds

P = 128
TILES = 5
GROUP = TILES * P
UNROLL = 5
WIN = 64
BLOCK = 500
SUB = 125
NJ = BLOCK // SUB
CHUNKS = 2 * UNROLL
CHUNK_TILES = ((0, 3), (3, 5))
EPS = 1e-5


class Names:
    pass


def wait_for(eng, sem, count):
    if isinstance(count, int) and count < 1:
        return
    eng.wait_ge(sem, count)


def edge_sweep(eng, step, total, unroll, lag):
    for i in range(2):
        for q in range(unroll):
            step(i, q)
    with eng.Fori(2, total // unroll) as i:
        for q in range(unroll):
            step(i, q)
    for q in range(lag):
        step(total // unroll, q)


def item(i, q, lag, unroll, total):
    if q < lag:
        i, q = i - 1, q + unroll
    n = i * unroll + q - lag
    if isinstance(n, int) and not 0 <= n < total:
        return None
    return n, i, q - lag


def node_sweep(eng, step, total, lag=0):
    peel = 5
    for n in range(peel):
        step(n, n % 2, n // 2)
    with eng.Fori(0, (total - peel) // 2) as i:
        for q in range(2):
            step(i * 2 + (peel + q), (peel + q) % 2, i + (peel + q) // 2)
    for n in range(total, total + lag):
        step(n, n % 2, n // 2)


def block_before(n, slot, turn, lag, total):
    m = n - lag
    if isinstance(m, int):
        return (m, m % 2, m // 2) if 0 <= m < total else None
    if lag % 2 == 0:
        return m, slot, turn - lag // 2
    return m, 1 - slot, turn - (lag + 1) // 2 + slot


def load_and_index(nc, m, d, t, sb, pb, sem):
    rows = m.E // SUB
    dst_i, src_i = sb("dst_i", [SUB, rows], I32), sb("src_i", [SUB, rows], I32)
    dst_f, src_f = sb("dst_f", [SUB, rows], FP32), sb("src_f", [SUB, rows], FP32)
    rest = sb("rest", [SUB, rows], FP32)
    parts = sb("parts", [SUB, 3, rows], BF16)
    wt_row = sb("wt_row", [1, P], FP32)
    wt_parts = sb("wt_parts", [1, 3, P], BF16)
    groups_row = rows // GROUP
    low = sb("low", [SUB, groups_row], FP32)
    span = sb("span", [SUB, groups_row], FP32)
    span_all = sb("span_all", [P, m.NG], FP32)
    widest = sb("widest", [P, 1], FP32)
    is_slow, is_fast = sb("is_slow", [P, 1], FP32), sb("is_fast", [P, 1], FP32)
    passes_f = sb("passes_f", [1, 1], FP32)
    iota_i, iota_f = sb("iota_i", [1, WIN], I32), sb("iota_f", [1, WIN], FP32)
    flip = [pb("flip0", [P, 512], FP32), pb("flip1", [P, 512], FP32)]
    dst_in, src_in, weight_in, params_in = sem("dst_in"), sem("src_in"), sem("weight_in"), sem("params_in")
    identity_ready, iota_ready, ones_ready = sem("identity_ready"), sem("iota_ready"), sem("ones_ready")
    dst_float, src_float = sem("dst_float"), sem("src_float")
    low_ready, parts_ready, wt_ready = sem("low_ready"), sem("parts_ready"), sem("wt_ready")
    low_stored, parts_stored, wt_stored = sem("low_stored"), sem("parts_stored"), sem("wt_stored")
    low_back, wt_back = sem("low_back"), sem("wt_back")
    flipped, flip_copied = sem("flipped"), sem("flip_copied")
    chain, pool_chain, act_zero = sem("chain"), sem("pool_chain"), sem("act_zero")
    iota_spread = sem("iota_spread")

    with nc.Block() as block:
        @block.sync
        def _(sp):
            sp.dma_start(dst_i[:], d["dst"].rearrange("(q r) -> q r", q=SUB)).then_inc(dst_in, 16)
            sp.dma_start(src_i[:], d["src"].rearrange("(q r) -> q r", q=SUB)).then_inc(src_in, 16)
            sp.dma_start(rest[:], d["edge_weight"].rearrange("(q r) -> q r", q=SUB)).then_inc(weight_in, 16)
            sp.dma_start(wt_row[:], d["Wt"]).then_inc(weight_in, 16)
            sp.wait_ge(low_ready, 1)
            sp.dma_start(d["low"].rearrange("(q k) -> q k", q=SUB), low[:]).then_inc(low_stored, 16)
            sp.dma_start(d["span"].rearrange("(q k) -> q k", q=SUB), span[:]).then_inc(low_stored, 16)
            sp.wait_ge(low_stored, 32)
            sp.dma_start(t.fast_base[:], d["low"].partition_broadcast(P)).then_inc(low_back, 16)
            sp.dma_start(span_all[:], d["span"].partition_broadcast(P)).then_inc(low_back, 16)
            sp.wait_ge(parts_ready, 1)
            sp.dma_start(d["weight_parts"].rearrange("c (q r) -> q c r", q=SUB), parts[:]).then_inc(parts_stored, 16)
            sp.wait_ge(wt_ready, 1)
            sp.dma_start(d["wt_parts"].rearrange("(o c) f -> o c f", o=1), wt_parts[:]).then_inc(wt_stored, 16)
            sp.wait_ge(wt_stored, 16)
            for c in range(3):
                sp.dma_start(t.Wt9[3 * c:3 * c + 3, :], d["wt_parts"]).then_inc(wt_back, 16)
            sp.wait_ge(wt_back, 48)
            sp.wait_ge(low_back, 32)
            sp.wait_ge(parts_stored, 16)

        @block.scalar
        def _(act):
            loads = [
                (t.We1[:], d["We1"]), (t.We2[:], d["We2"]), (t.Wm_x[:], d["Wm1"][0:P, :]), (t.Wm_e[:], d["Wm1"][P:2 * P, :]),
                (t.Wm2[:], d["Wm2"]), (t.Ws1[:], d["Ws1"]), (t.Wn1[:], d["Wn1"]),
                (t.Wn2a[:], d["Wn2"][0:P, :]), (t.Wn2b[:], d["Wn2"][P:m.H, :]),
                (t.Ws2a[:], d["Ws2"][0:P, :]), (t.Ws2b[:], d["Ws2"][P:m.H, :]),
                (t.b1a[:], d["b1"][0:P].rearrange("(f o) -> f o", o=1)), (t.b1b[:], d["b1"][P:m.H].rearrange("(f o) -> f o", o=1)),
                (t.be1[:], d["be1"].rearrange("(f o) -> f o", o=1)), (t.be2[:], d["be2"].rearrange("(f o) -> f o", o=1)),
                (t.bt[:], d["bt"].rearrange("(f o) -> f o", o=1)),
                (t.b2[:], d["b2"].partition_broadcast(P)), (t.bm1[:], d["bm1"].partition_broadcast(P)),
                (t.bm2[:], d["bm2"].partition_broadcast(P)),
            ]
            for out, in_ in loads:
                act.dma_start(out, in_).then_inc(params_in, 16)
            act.wait_ge(params_in, 16 * len(loads))

        @block.gpsimd
        def _(pool):
            nc.gpsimd.memset(t.identity[:], 0.0).then_inc(pool_chain, 1)
            pool.wait_ge(pool_chain, 1)
            nc.gpsimd.affine_select(out=t.identity[:], in_=t.identity[:], compare_op=ALU.not_equal, fill=1.0,
                                    base=0, pattern=[[-1, P]], channel_multiplier=1).then_inc(identity_ready, 1)
            nc.gpsimd.iota(iota_i[:], pattern=[[1, WIN]], base=0, channel_multiplier=0).then_inc(iota_ready, 1)
            nc.gpsimd.memset(t.ones[:], 1.0).then_inc(ones_ready, 1)
            nc.gpsimd.memset(t.ones_row[:], 1.0).then_inc(ones_ready, 1)
            nc.gpsimd.memset(t.eps[:], EPS).then_inc(ones_ready, 1)

        @block.vector
        def _(dve):
            done = [0]

            def then(ins):
                done[0] += 1
                ins.then_inc(chain, 1)
                dve.wait_ge(chain, done[0])

            dve.wait_ge(dst_in, 16)
            nc.vector.tensor_copy(dst_f[:], dst_i[:]).then_inc(dst_float, 1)
            dve.wait_ge(src_in, 16)
            nc.vector.tensor_copy(src_f[:], src_i[:]).then_inc(src_float, 1)
            dve.wait_ge(iota_ready, 1)
            then(nc.vector.tensor_copy(iota_f[:], iota_i[:]))
            dve.wait_ge(dst_float, 1)
            by_group = dst_f[:].rearrange("q (k e) -> q k e", e=GROUP)
            then(nc.vector.tensor_reduce(low[:], by_group, axis=AX.X, op=ALU.min))
            then(nc.vector.tensor_reduce(span[:], by_group, axis=AX.X, op=ALU.max))
            nc.vector.tensor_tensor(span[:], span[:], low[:], ALU.subtract).then_inc(low_ready, 1)
            dve.wait_ge(weight_in, 32)
            for left, cut, ready in ((wt_row[:], wt_parts, wt_ready), (rest[:], parts, parts_ready)):
                then(nc.vector.tensor_copy(cut[:, 0, :], left))
                then(nc.vector.tensor_tensor(left, left, cut[:, 0, :], ALU.subtract))
                then(nc.vector.tensor_copy(cut[:, 1, :], left))
                then(nc.vector.tensor_tensor(left, left, cut[:, 1, :], ALU.subtract))
                nc.vector.tensor_copy(cut[:, 2, :], left).then_inc(ready, 1)
            n = 0
            for out in (t.rel, t.src_idx):
                for k in range(groups_row):
                    for j in range(TILES):
                        dve.wait_ge(flipped, n + 1)
                        nc.vector.tensor_copy(out[:].rearrange("p (q k) j -> p q k j", k=groups_row)[:, :, k, j],
                                              flip[n % 2][:, 0:SUB]).then_inc(flip_copied, 1)
                        n += 1
            dve.wait_ge(low_back, 32)
            then(nc.vector.tensor_reduce(widest[:], span_all[:], axis=AX.X, op=ALU.max))
            then(nc.vector.tensor_scalar(is_slow[:], widest[:], float(WIN), None, ALU.is_ge))
            then(nc.vector.tensor_scalar(is_fast[:], widest[:], float(WIN), None, ALU.is_lt))
            then(nc.vector.tensor_scalar(t.window_step[:], is_slow[:], float(WIN), None, ALU.mult))
            then(nc.vector.tensor_scalar(t.fast_base[:], t.fast_base[:], is_fast[:, 0:1], None, ALU.mult))
            then(nc.vector.tensor_scalar(passes_f[:], is_slow[0:1, :], float(m.WINDOWS - 1), 1.0, ALU.mult, ALU.add))
            then(nc.vector.tensor_copy(t.passes[:], passes_f[:]))
            then(nc.vector.memset(t.base_now[:], 0.0))
            then(nc.vector.memset(t.slow_base[:], 0.0))

        @block.tensor
        def _(pe):
            pe.wait_ge(identity_ready, 1)
            n = 0
            for src, ready in ((dst_f, dst_float), (src_f, src_float)):
                pe.wait_ge(ready, 1)
                by_tile = src[:].rearrange("q (k p j) -> q k j p", p=P, j=TILES)
                for k in range(groups_row):
                    for j in range(TILES):
                        if n >= 2:
                            pe.wait_ge(flip_copied, n - 1)
                        nc.tensor.transpose(flip[n % 2][:, 0:SUB], by_tile[:, k, j, :],
                                            t.identity[0:SUB, 0:SUB]).then_inc(flipped, 1)
                        n += 1
            pe.wait_ge(ones_ready, 3)
            pe.wait_ge(chain, 1)
            nc.tensor.matmul(t.iota_ps[:, 0:WIN], t.ones_row[:], iota_f[:], start=True, stop=True).then_inc(iota_spread, 1)


def set_windows(nc, dve, m, t, chain, base_ready):
    done = [0]

    def then(ins):
        done[0] += 1
        ins.then_inc(chain, 1)
        dve.wait_ge(chain, done[0])

    then(nc.vector.tensor_scalar(t.base_next[:], t.fast_base[:], t.slow_base[:, 0:1], None, ALU.add))
    then(nc.vector.tensor_tensor(t.base_now[:], t.base_now[:], t.base_next[:], ALU.subtract))
    then(nc.vector.tensor_tensor(t.rel[:], t.rel[:], t.base_now[:].unsqueeze(2).to_broadcast([P, m.NG, TILES]), ALU.add))
    then(nc.vector.tensor_copy(t.base_now[:], t.base_next[:]))
    then(nc.vector.tensor_tensor(t.slow_base[:], t.slow_base[:], t.window_step[:], ALU.add))
    nc.vector.tensor_copy(t.base_int[:], t.base_next[0:1, :]).then_inc(base_ready, 1)
    dve.wait_ge(base_ready, 1)


def one_hot(nc, t, hot, g, slot):
    return nc.vector.tensor_tensor(
        hot[:, slot],
        t.iota_ps[:, 0:WIN].unsqueeze(1).to_broadcast([P, TILES, WIN]),
        t.rel[:, ds(g, 1), :].rearrange("p o j -> p (o j)").unsqueeze(2).to_broadcast([P, TILES, WIN]), ALU.is_equal)


def gather_groups(nc, pool, m, table, idx, rows, idx_loaded, sums_ready, gathers_started, rows_arrived):
    def step(i, q):
        g = i * UNROLL + q
        wait_for(pool, sums_ready, g - UNROLL + 1)
        pool.wait_ge(idx_loaded, g + 1)
        pool.sem_inc(gathers_started, 1)
        for j in range(TILES):
            nc.gpsimd.indirect_dma_start(
                out=rows[:, q, j, :], out_offset=None, in_=table,
                in_offset=bass.IndirectOffsetOnAxis(ap=idx[:, q, j:j + 1], axis=0)).then_inc(rows_arrived[q][j], 16)
    edge_sweep(pool, step, m.NG, UNROLL, 0)
    for slot in rows_arrived:
        for tile_arrived in slot:
            pool.wait_ge(tile_arrived, m.NG // UNROLL * 16)


def clear_counts(nc, sems, gathered=False):
    if gathered:
        nc.gpsimd.dma_reset()
    for s in sems:
        nc.gpsimd.sem_clear(s)
    nc.all_engine_barrier()


def sum_neighbours(nc, m, t, table, degree, sb, pb, sem):
    idx = sb("idx", [P, UNROLL, TILES], I32)
    rows = sb("rows", [P, UNROLL, TILES, P], FP32)
    hot = sb("hot", [P, UNROLL, TILES, WIN], FP32)
    bank = (0, 1, 0, 1, 2)
    win = [pb(f"win{b}", [P, 512], FP32) for b in range(3)]
    cnt = [pb(f"cnt{b}", [P, 512], FP32) for b in range(3)] if degree is not None else []
    idx_loaded, gathers_started = sem("idx_loaded"), sem("gathers_started")
    rows_arrived = [[sem(f"rows_arrived{q}_{j}") for j in range(TILES)] for q in range(UNROLL)]
    hot_ready, sums_ready, window_added = sem("hot_ready"), sem("sums_ready"), sem("window_added")
    chain, base_ready = sem("chain"), sem("base_ready")
    sems = [idx_loaded, gathers_started, *[a for slot in rows_arrived for a in slot], hot_ready, sums_ready, window_added, chain, base_ready]

    def one_pass():
        with nc.Block() as block:
            @block.gpsimd
            def _(pool):
                gather_groups(nc, pool, m, table, idx, rows, idx_loaded, sums_ready, gathers_started, rows_arrived)

            @block.scalar
            def _(act):
                def step(i, q):
                    g = i * UNROLL + q
                    wait_for(act, sums_ready, g - UNROLL + 1)
                    nc.scalar.copy(idx[:, q, :], t.src_idx[:, ds(g, 1), :].rearrange("p o j -> p (o j)")).then_inc(idx_loaded, 1)
                edge_sweep(act, step, m.NG, UNROLL, 0)

            @block.vector
            def _(dve):
                set_windows(nc, dve, m, t, chain, base_ready)

                def step(i, q):
                    now = item(i, q, 0, UNROLL, m.NG)
                    if now:
                        g, _, slot = now
                        wait_for(dve, sums_ready, g - UNROLL + 1)
                        one_hot(nc, t, hot, g, slot).then_inc(hot_ready, 1)
                    late = item(i, q, 2, UNROLL, m.NG)
                    if late:
                        g, _, slot = late
                        base = dve.value_load(t.base_int[0:1, ds(g, 1)], min_val=0, max_val=m.N)
                        wait_for(dve, window_added, g)
                        dve.wait_ge(sums_ready, g + 1)
                        w = ds(base, WIN)
                        if degree is not None:
                            nc.vector.tensor_tensor(degree[:, w], degree[:, w], cnt[bank[slot]][0:1, 0:WIN], ALU.add)
                        nc.vector.tensor_tensor(t.sums[:, w], t.sums[:, w], win[bank[slot]][:, 0:WIN],
                                                ALU.add).then_inc(window_added, 1)
                edge_sweep(dve, step, m.NG, UNROLL, 2)

            @block.tensor
            def _(pe):
                def step(i, q):
                    g = i * UNROLL + q
                    wait_for(pe, window_added, g - 1)
                    pe.wait_ge(hot_ready, g + 1)
                    for j in range(TILES):
                        pe.wait_ge(rows_arrived[q][j], i * 16 + 16)
                    for j in range(TILES):
                        last = nc.tensor.matmul(win[bank[q]][:, 0:WIN], rows[:, q, j, :], hot[:, q, j, :],
                                                start=j == 0, stop=j == TILES - 1)
                    if degree is not None:
                        for j in range(TILES):
                            last = nc.tensor.matmul(cnt[bank[q]][0:1, 0:WIN], t.ones[:], hot[:, q, j, :],
                                                    start=j == 0, stop=j == TILES - 1)
                    last.then_inc(sums_ready, 1)
                edge_sweep(pe, step, m.NG, UNROLL, 0)

            @block.sync
            def _(sp):
                sp.wait_ge(window_added, m.NG)
        clear_counts(nc, sems, gathered=True)

    all_passes(nc, m, t, one_pass)


def all_passes(nc, m, t, one_pass):
    passes = nc.values_load(t.passes[0:1, 0:1], min_val=1, max_val=m.WINDOWS)
    with nc.Fori(0, m.WINDOWS, m.PASS_STRIDE) as outer:
        with nc.If(outer < passes):
            with nc.Fori(0, m.PASS_STRIDE) as inner:
                with nc.If(outer + inner < passes):
                    one_pass()


def clear_sums(nc, t, more=()):
    with nc.Block() as block:
        @block.vector
        def _(dve):
            nc.vector.memset(t.sums[:], 0.0)
            nc.vector.memset(t.slow_base[:], 0.0)
            for x in more:
                nc.vector.memset(x, 0.0)


def mean_block(nc, pool, t, mean, inv, n, slot):
    return nc.gpsimd.tensor_tensor(mean[:, slot], t.sums[:, ds(n * BLOCK, BLOCK)].rearrange("f (p j) -> f j p", j=NJ),
                                   inv[:, slot].rearrange("f (p j) -> f j p", j=NJ), ALU.mult)


def node_rows(ap, n):
    return ap.rearrange("(b p j) f -> b p (j f)", p=SUB, j=NJ)[ds(n, 1), :, :].rearrange("o p c -> (o p) c")


def invert_degrees(nc, m, d, t, degree, sb, pb, sem):
    stored, back, inv_ready, inv_stored, chain = sem("stored"), sem("back"), sem("inv_ready"), sem("inv_stored"), sem("chain")
    with nc.Block() as block:
        @block.sync
        def _(sp):
            sp.dma_start(d["degree"].rearrange("(o n) -> o n", o=1), degree[:, 0:m.N]).then_inc(stored, 16)
            sp.wait_ge(stored, 16)
            sp.dma_start(t.degree_n[:], d["degree"].rearrange("(b p j) -> p b j", p=SUB, j=NJ)).then_inc(back, 16)
            sp.wait_ge(inv_ready, 1)
            sp.dma_start(d["inv_degree"].rearrange("(b p j) -> p b j", p=SUB, j=NJ), t.inv_n[:]).then_inc(inv_stored, 16)
            sp.wait_ge(inv_stored, 16)

        @block.vector
        def _(dve):
            done = [0]

            def then(ins):
                done[0] += 1
                ins.then_inc(chain, 1)
                dve.wait_ge(chain, done[0])

            dve.wait_ge(back, 16)
            then(nc.vector.tensor_scalar(t.inv_n[:], t.degree_n[:], 1.0, None, ALU.max))
            then(nc.vector.reciprocal(t.inv_n[:], t.inv_n[:]))
            then(nc.vector.tensor_scalar(t.has_n[:], t.degree_n[:], 0.0, None, ALU.is_gt))
            nc.vector.tensor_tensor(t.inv_n[:], t.inv_n[:], t.has_n[:], ALU.mult).then_inc(inv_ready, 1)


def first_nodes(nc, m, d, t, sb, pb, sem):
    x = sb("x", [SUB, 2, NJ * P], FP32)
    inv = sb("inv", [P, 2, BLOCK], FP32)
    mean = sb("mean", [P, 2, NJ, SUB], FP32)
    xb = sb("xb", [SUB, 2, NJ, P], FP32)
    xT = sb("xT", [P, 2, BLOCK], FP32)
    hA, hB = sb("hA", [P, 2, NJ, SUB], FP32), sb("hB", [m.H - P, 2, NJ, SUB], FP32)
    z, own = sb("z", [SUB, 2, NJ * P], FP32), sb("own", [SUB, 2, NJ * P], FP32)
    p_x, p_hA, p_hB = pb("p_x", [P, 512], FP32), pb("p_hA", [P, 512], FP32), pb("p_hB", [P, 512], FP32)
    p_z, p_own = pb("p_z", [P, 512], FP32), pb("p_own", [P, 512], FP32)
    x_in, inv_in = [sem("x_in0"), sem("x_in1")], [sem("inv_in0"), sem("inv_in1")]
    z_out, own_out = [sem("z_out0"), sem("z_out1")], [sem("own_out0"), sem("own_out1")]
    mean_ready, xb_ready, x_flipped, x_copied = sem("mean_ready"), sem("xb_ready"), sem("x_flipped"), sem("x_copied")
    h_summed, h_ready, out_summed = sem("h_summed"), sem("h_ready"), sem("out_summed")
    z_ready, own_ready = sem("z_ready"), sem("own_ready")

    with nc.Block() as block:
        @block.sync
        def _(sp):
            def step(n, slot, turn):
                now = block_before(n, slot, turn, 0, m.NB)
                if now:
                    wait_for(sp, x_flipped, n - 1)
                    wait_for(sp, xb_ready, n - 1)
                    wait_for(sp, mean_ready, n - 1)
                    sp.dma_start(x[:, slot], node_rows(d["x"], n)).then_inc(x_in[slot], 16)
                    sp.dma_start(inv[:, slot], d["inv_degree"][ds(n * BLOCK, BLOCK)].partition_broadcast(P)).then_inc(inv_in[slot], 16)
                late = block_before(n, slot, turn, 3, m.NB)
                if late:
                    n, slot, turn = late
                    sp.wait_ge(z_ready, n + 1)
                    sp.dma_start(node_rows(d["z"], n), z[:, slot]).then_inc(z_out[slot], 16)
                    sp.wait_ge(own_ready, n + 1)
                    sp.dma_start(node_rows(d["own"], n), own[:, slot]).then_inc(own_out[slot], 16)
            node_sweep(sp, step, m.NB, 3)
            for slot in range(2):
                uses = (m.NB + 1 - slot) // 2
                sp.wait_ge(z_out[slot], 16 * uses)
                sp.wait_ge(own_out[slot], 16 * uses)

        @block.gpsimd
        def _(pool):
            def step(n, slot, turn):
                pool.wait_ge(inv_in[slot], turn * 16 + 16)
                wait_for(pool, h_summed, n - 1)
                mean_block(nc, pool, t, mean, inv, n, slot).then_inc(mean_ready, 1)
                pool.wait_ge(x_in[slot], turn * 16 + 16)
                wait_for(pool, own_ready, n - 1)
                nc.gpsimd.tensor_tensor(xb[:, slot], x[:, slot].rearrange("p (j f) -> p j f", j=NJ),
                                        t.b2[0:SUB, :].unsqueeze(1).to_broadcast([SUB, NJ, P]), ALU.add).then_inc(xb_ready, 1)
            node_sweep(pool, step, m.NB)

        @block.tensor
        def _(pe):
            def step(n, slot, turn):
                now = block_before(n, slot, turn, 0, m.NB)
                if now:
                    b, s, use = now
                    pe.wait_ge(x_in[s], use * 16 + 16)
                    wait_for(pe, x_copied, b)
                    for j in range(NJ):
                        last = nc.tensor.transpose(p_x[:, j * SUB:(j + 1) * SUB], x[:, s, j * P:(j + 1) * P],
                                                   t.identity[0:SUB, 0:SUB])
                    last.then_inc(x_flipped, 1)
                mid = block_before(n, slot, turn, 1, m.NB)
                if mid:
                    b, s, _ = mid
                    pe.wait_ge(x_copied, b + 1)
                    pe.wait_ge(mean_ready, b + 1)
                    wait_for(pe, h_ready, b)
                    for bank, k0, k1 in ((p_hA, 0, P), (p_hB, P, m.H)):
                        out = bank[0:k1 - k0, 0:BLOCK]
                        nc.tensor.matmul(out, t.Ws1[:, k0:k1], xT[:, s, :], start=True, stop=False)
                        last = nc.tensor.matmul(out, t.Wn1[:, k0:k1], mean[:, s].rearrange("f j p -> f (j p)"),
                                                start=False, stop=True)
                    last.then_inc(h_summed, 1)
                late = block_before(n, slot, turn, 2, m.NB)
                if late:
                    b, s, _ = late
                    pe.wait_ge(h_ready, b + 1)
                    wait_for(pe, z_ready, b)
                    wait_for(pe, own_ready, b)
                    for bank, wa, wb in ((p_z, t.Wn2a, t.Wn2b), (p_own, t.Ws2a, t.Ws2b)):
                        for j in range(NJ):
                            out = bank[0:SUB, j * P:(j + 1) * P]
                            nc.tensor.matmul(out, hA[:, s, j, :], wa[:], start=True, stop=False)
                            last = nc.tensor.matmul(out, hB[:, s, j, :], wb[:], start=False, stop=True)
                    last.then_inc(out_summed, 1)
            node_sweep(pe, step, m.NB, 2)

        @block.scalar
        def _(act):
            def step(n, slot, turn):
                now = block_before(n, slot, turn, 0, m.NB)
                if now:
                    b, s, _ = now
                    act.wait_ge(x_flipped, b + 1)
                    wait_for(act, h_summed, b - 1)
                    nc.scalar.copy(xT[:, s, :], p_x[:, 0:BLOCK]).then_inc(x_copied, 1)
                mid = block_before(n, slot, turn, 1, m.NB)
                if mid:
                    b, s, _ = mid
                    act.wait_ge(h_summed, b + 1)
                    wait_for(act, out_summed, b - 1)
                    nc.scalar.activation(hA[:, s].rearrange("f j p -> f (j p)"), p_hA[:, 0:BLOCK], ACT.Relu, bias=t.b1a[:, 0:1])
                    nc.scalar.activation(hB[:, s].rearrange("f j p -> f (j p)"), p_hB[0:m.H - P, 0:BLOCK], ACT.Relu,
                                         bias=t.b1b[:, 0:1]).then_inc(h_ready, 1)
                late = block_before(n, slot, turn, 2, m.NB)
                if late:
                    b, s, use = late
                    act.wait_ge(out_summed, b + 1)
                    wait_for(act, z_out[s], use * 16)
                    nc.scalar.copy(z[:, s, :], p_z[0:SUB, :]).then_inc(z_ready, 1)
            node_sweep(act, step, m.NB, 2)

        @block.vector
        def _(dve):
            def step(n, slot, turn):
                late = block_before(n, slot, turn, 2, m.NB)
                if late:
                    b, s, use = late
                    dve.wait_ge(out_summed, b + 1)
                    dve.wait_ge(xb_ready, b + 1)
                    wait_for(dve, own_out[s], use * 16)
                    nc.vector.tensor_tensor(own[:, s, :], p_own[0:SUB, :], xb[:, s].rearrange("p j f -> p (j f)"),
                                            ALU.add).then_inc(own_ready, 1)
            node_sweep(dve, step, m.NB, 2)


def norm_buffers(sb, sem):
    k = Names()
    k.u, k.normed = sb("u", [SUB, 2, NJ, P], FP32), sb("normed", [SUB, 2, NJ, P], FP32)
    k.stats, k.moments = sb("stats", [SUB, 2, NJ, 6], FP32), sb("moments", [SUB, 2, NJ, 2], FP32)
    k.std, k.scale = sb("std", [SUB, 2, NJ], FP32), sb("scale", [SUB, 2, NJ], FP32)
    k.u_ready, k.stats_ready, k.aggregates_started = sem("u_ready"), sem("stats_ready"), sem("aggregates_started")
    k.moments_ready, k.std_ready, k.scale_ready = sem("moments_ready"), sem("std_ready"), sem("scale_ready")
    k.normed_ready = sem("normed_ready")
    return k


def norm_moments(nc, dve, k, b, s):
    dve.wait_ge(k.u_ready, b + 1)
    for j in range(NJ):
        last = nc.vector.bn_stats(k.stats[:, s, j, :], k.u[:, s, j, :])
    last.then_inc(k.stats_ready, 1)
    dve.wait_ge(k.stats_ready, b + 1)
    dve.sem_inc(k.aggregates_started, 1)
    for j in range(NJ):
        last = nc.vector.bn_aggr(k.moments[:, s, j, :], k.stats[:, s, j, :])
    last.then_inc(k.moments_ready, 1)


def norm_std(nc, act, t, k, b, s):
    act.wait_ge(k.moments_ready, b + 1)
    nc.scalar.activation(k.std[:, s, :], k.moments[:, s, :, 1], ACT.Sqrt, bias=t.eps[0:SUB, 0:1]).then_inc(k.std_ready, 1)


def norm_apply(nc, dve, k, b, s):
    dve.wait_ge(k.std_ready, b + 1)
    nc.vector.reciprocal(k.scale[:, s, :], k.std[:, s, :]).then_inc(k.scale_ready, 1)
    dve.wait_ge(k.scale_ready, b + 1)
    for j in range(NJ):
        last = nc.vector.tensor_scalar(k.normed[:, s, j, :], k.u[:, s, j, :], k.moments[:, s, j, 0:1],
                                       k.scale[:, s, j:j + 1], ALU.subtract, ALU.mult)
    last.then_inc(k.normed_ready, 1)


def second_nodes(nc, m, d, t, sb, pb, sem):
    own = sb("own", [SUB, 2, NJ * P], FP32)
    inv = sb("inv", [P, 2, BLOCK], FP32)
    mean = sb("mean", [P, 2, NJ, SUB], FP32)
    x1T = sb("x1T", [P, 2, NJ, SUB], FP32)
    y = sb("y", [SUB, 2, NJ, P], FP32)
    p_mean, p_x1, p_y = pb("p_mean", [P, 512], FP32), pb("p_x1", [P, 512], FP32), pb("p_y", [P, 512], FP32)
    k = norm_buffers(sb, sem)
    own_in, inv_in = [sem("own_in0"), sem("own_in1")], [sem("inv_in0"), sem("inv_in1")]
    x1_out, y_out = [sem("x1_out0"), sem("x1_out1")], [sem("y_out0"), sem("y_out1")]
    mean_ready, mean_flipped, x1_flipped, x1_copied = sem("mean_ready"), sem("mean_flipped"), sem("x1_flipped"), sem("x1_copied")
    y_summed, y_ready = sem("y_summed"), sem("y_ready")

    with nc.Block() as block:
        @block.sync
        def _(sp):
            def step(n, slot, turn):
                now = block_before(n, slot, turn, 0, m.NB)
                if now:
                    wait_for(sp, k.u_ready, n - 1)
                    wait_for(sp, mean_ready, n - 1)
                    sp.dma_start(own[:, slot], node_rows(d["own"], n)).then_inc(own_in[slot], 16)
                    sp.dma_start(inv[:, slot], d["inv_degree"][ds(n * BLOCK, BLOCK)].partition_broadcast(P)).then_inc(inv_in[slot], 16)
                late = block_before(n, slot, turn, 2, m.NB)
                if late:
                    b, s, _ = late
                    sp.wait_ge(k.normed_ready, b + 1)
                    sp.dma_start(node_rows(d["x1"], b), k.normed[:, s].rearrange("p j f -> p (j f)")).then_inc(x1_out[s], 16)
                last = block_before(n, slot, turn, 4, m.NB)
                if last:
                    b, s, _ = last
                    sp.wait_ge(y_ready, b + 1)
                    sp.dma_start(node_rows(d["y"], b), y[:, s].rearrange("p j f -> p (j f)")).then_inc(y_out[s], 16)
            node_sweep(sp, step, m.NB, 4)
            for slot in range(2):
                uses = (m.NB + 1 - slot) // 2
                sp.wait_ge(x1_out[slot], 16 * uses)
                sp.wait_ge(y_out[slot], 16 * uses)

        @block.gpsimd
        def _(pool):
            def step(n, slot, turn):
                pool.wait_ge(inv_in[slot], turn * 16 + 16)
                wait_for(pool, mean_flipped, n - 1)
                mean_block(nc, pool, t, mean, inv, n, slot).then_inc(mean_ready, 1)
            node_sweep(pool, step, m.NB)

        @block.tensor
        def _(pe):
            def step(n, slot, turn):
                now = block_before(n, slot, turn, 0, m.NB)
                if now:
                    b, s, _ = now
                    pe.wait_ge(mean_ready, b + 1)
                    wait_for(pe, k.u_ready, b)
                    for j in range(NJ):
                        last = nc.tensor.transpose(p_mean[0:SUB, j * P:(j + 1) * P], mean[:, s, j, :], t.identity[:])
                    last.then_inc(mean_flipped, 1)
                mid = block_before(n, slot, turn, 1, m.NB)
                if mid:
                    b, s, _ = mid
                    pe.wait_ge(k.normed_ready, b + 1)
                    wait_for(pe, x1_copied, b)
                    for j in range(NJ):
                        last = nc.tensor.transpose(p_x1[:, j * SUB:(j + 1) * SUB], k.normed[:, s, j, :],
                                                   t.identity[0:SUB, 0:SUB])
                    last.then_inc(x1_flipped, 1)
                late = block_before(n, slot, turn, 2, m.NB)
                if late:
                    b, s, _ = late
                    pe.wait_ge(x1_copied, b + 1)
                    wait_for(pe, y_ready, b)
                    for j in range(NJ):
                        last = nc.tensor.matmul(p_y[0:SUB, j * P:(j + 1) * P], x1T[:, s, j, :], t.Wm_x[:],
                                                start=True, stop=True)
                    last.then_inc(y_summed, 1)
            node_sweep(pe, step, m.NB, 2)

        @block.scalar
        def _(act):
            def step(n, slot, turn):
                now = block_before(n, slot, turn, 0, m.NB)
                if now:
                    norm_std(nc, act, t, k, now[0], now[1])
                mid = block_before(n, slot, turn, 1, m.NB)
                if mid:
                    b, s, _ = mid
                    act.wait_ge(x1_flipped, b + 1)
                    wait_for(act, y_summed, b - 1)
                    nc.scalar.copy(x1T[:, s].rearrange("f j p -> f (j p)"), p_x1[:, 0:BLOCK]).then_inc(x1_copied, 1)
            node_sweep(act, step, m.NB, 1)

        @block.vector
        def _(dve):
            def step(n, slot, turn):
                now = block_before(n, slot, turn, 0, m.NB)
                if now:
                    b, s, use = now
                    dve.wait_ge(own_in[s], use * 16 + 16)
                    dve.wait_ge(mean_flipped, b + 1)
                    wait_for(dve, k.normed_ready, b - 1)
                    nc.vector.tensor_tensor(k.u[:, s].rearrange("p j f -> p (j f)"), p_mean[0:SUB, :], own[:, s, :],
                                            ALU.add).then_inc(k.u_ready, 1)
                    norm_moments(nc, dve, k, b, s)
                late = block_before(n, slot, turn, 3, m.NB)
                if late:
                    b, s, use = late
                    dve.wait_ge(y_summed, b + 1)
                    wait_for(dve, y_out[s], use * 16)
                    nc.vector.tensor_tensor(y[:, s], p_y[0:SUB, :].rearrange("p (j f) -> p j f", j=NJ),
                                            t.bm1[0:SUB, :].unsqueeze(1).to_broadcast([SUB, NJ, P]),
                                            ALU.add).then_inc(y_ready, 1)
                if now:
                    b, s, use = now
                    wait_for(dve, x1_out[s], use * 16)
                    wait_for(dve, x1_flipped, b - 1)
                    norm_apply(nc, dve, k, b, s)
            node_sweep(dve, step, m.NB, 3)


def third_nodes(nc, m, d, t, sb, pb, sem):
    x1 = sb("x1", [SUB, 2, NJ, P], FP32)
    total = sb("total", [P, 2, NJ, SUB], FP32)
    bias = sb("bias", [SUB, 2, NJ, P], FP32)
    twice = sb("twice", [SUB, 2, NJ, P], FP32)
    base = sb("base", [SUB, 2, NJ, P], FP32)
    p_out = [pb("p_out0", [P, 512], FP32), pb("p_out1", [P, 512], FP32)]
    k = norm_buffers(sb, sem)
    x1_in, stored = [sem("x1_in0"), sem("x1_in1")], [sem("stored0"), sem("stored1")]
    total_ready, bias_ready, base_ready, out_summed = sem("total_ready"), sem("bias_ready"), sem("base_ready"), sem("out_summed")
    k.twice_ready = sem("twice_ready")

    with nc.Block() as block:
        @block.sync
        def _(sp):
            def step(n, slot, turn):
                now = block_before(n, slot, turn, 0, m.NB)
                if now:
                    wait_for(sp, k.u_ready, n - 1)
                    sp.dma_start(x1[:, slot].rearrange("p j f -> p (j f)"), node_rows(d["x1"], n)).then_inc(x1_in[slot], 16)
                late = block_before(n, slot, turn, 2, m.NB)
                if late:
                    b, s, _ = late
                    sp.wait_ge(k.normed_ready, b + 1)
                    sp.dma_start(node_rows(d["out"], b), k.normed[:, s].rearrange("p j f -> p (j f)")).then_inc(stored[s], 16)
            node_sweep(sp, step, m.NB, 2)
            for slot in range(2):
                sp.wait_ge(stored[slot], 16 * ((m.NB + 1 - slot) // 2))

        @block.gpsimd
        def _(pool):
            def step(n, slot, turn):
                wait_for(pool, k.u_ready, n - 1)
                nc.gpsimd.tensor_tensor(bias[:, slot], t.bm2[0:SUB, :].unsqueeze(1).to_broadcast([SUB, NJ, P]),
                                        t.degree_n[:, ds(n, 1), :].rearrange("p o j -> p (o j)").unsqueeze(2).to_broadcast([SUB, NJ, P]),
                                        ALU.mult).then_inc(bias_ready, 1)
                pool.wait_ge(x1_in[slot], turn * 16 + 16)
                pool.wait_ge(bias_ready, n + 1)
                nc.gpsimd.tensor_tensor(base[:, slot], x1[:, slot], bias[:, slot], ALU.add).then_inc(base_ready, 1)
            node_sweep(pool, step, m.NB)

        @block.scalar
        def _(act):
            def step(n, slot, turn):
                now = block_before(n, slot, turn, 0, m.NB)
                if now:
                    b, s, use = now
                    wait_for(act, out_summed, b - 1)
                    nc.scalar.copy(total[:, s], t.sums[:, ds(b * BLOCK, BLOCK)].rearrange("f (p j) -> f j p", j=NJ)
                                   ).then_inc(total_ready, 1)
                mid = block_before(n, slot, turn, 1, m.NB)
                if mid:
                    norm_std(nc, act, t, k, mid[0], mid[1])
            node_sweep(act, step, m.NB, 1)

        @block.tensor
        def _(pe):
            def step(n, slot, turn):
                pe.wait_ge(total_ready, n + 1)
                wait_for(pe, k.u_ready, n - 1)
                for j in range(NJ):
                    last = nc.tensor.matmul(p_out[slot][0:SUB, j * P:(j + 1) * P], total[:, slot, j, :], t.Wm2[:],
                                            start=True, stop=True)
                last.then_inc(out_summed, 1)
            node_sweep(pe, step, m.NB)

        @block.vector
        def _(dve):
            def step(n, slot, turn):
                now = block_before(n, slot, turn, 0, m.NB)
                if now:
                    b, s, use = now
                    dve.wait_ge(out_summed, b + 1)
                    dve.wait_ge(base_ready, b + 1)
                    wait_for(dve, k.normed_ready, b - 1)
                    dve.wait_ge(x1_in[s], use * 16 + 16)
                    nc.vector.tensor_tensor(twice[:, s].rearrange("p j f -> p (j f)"), p_out[s][0:SUB, :],
                                            base[:, s].rearrange("p j f -> p (j f)"), ALU.add).then_inc(k.twice_ready, 1)
                    dve.wait_ge(k.twice_ready, b + 1)
                    nc.vector.tensor_tensor(k.u[:, s], twice[:, s], x1[:, s], ALU.add).then_inc(k.u_ready, 1)
                    norm_moments(nc, dve, k, b, s)
                late = block_before(n, slot, turn, 1, m.NB)
                if late:
                    b, s, use = late
                    wait_for(dve, stored[s], use * 16)
                    norm_apply(nc, dve, k, b, s)
            node_sweep(dve, step, m.NB, 1)


def sum_messages(nc, m, d, t, sb, pb, sem):
    A = d["attr"].shape[1]
    idx = sb("idx", [P, UNROLL, TILES], I32)
    rows = sb("rows", [P, UNROLL, TILES, P], FP32)
    hot = sb("hot", [P, UNROLL, TILES, WIN], FP32)
    attr = sb("attr", [P, UNROLL, TILES, A], FP32)
    when = sb("when", [9, UNROLL, GROUP], BF16)
    wide = 3 * P
    attrT = sb("attrT", [A, 2, wide], FP32)
    hid = sb("hid", [P, 2, wide], FP32)
    gate = sb("gate", [P, 2, wide], FP32)
    gated = sb("gated", [P, 2, wide], FP32)
    p_attr, p_hid, p_edge = pb("p_attr", [P, 512], FP32), pb("p_hid", [P, 512], FP32), pb("p_edge", [P, 512], FP32)
    p_time, p_msg = pb("p_time", [P, 512], FP32), pb("p_msg", [P, 512], FP32)
    win = [pb("win0", [P, 512], FP32), pb("win1", [P, 512], FP32)]
    idx_loaded, gathers_started = sem("idx_loaded"), sem("gathers_started")
    rows_arrived = [[sem(f"rows_arrived{q}_{j}") for j in range(TILES)] for q in range(UNROLL)]
    attr_arrived = [sem(f"attr_arrived{q}") for q in range(UNROLL)]
    when_arrived = [sem(f"when_arrived{q}") for q in range(UNROLL)]
    hot_ready, sums_ready, window_added = sem("hot_ready"), sem("sums_ready"), sem("window_added")
    chain, base_ready = sem("chain"), sem("base_ready")
    attr_flipped, attr_copied = sem("attr_flipped"), sem("attr_copied")
    hid_summed, hid_ready = sem("hid_summed"), sem("hid_ready")
    edge_summed, time_summed, gate_ready, gated_ready = sem("edge_summed"), sem("time_summed"), sem("gate_ready"), sem("gated_ready")
    msg_summed, msg_added, msg_ready = sem("msg_summed"), sem("msg_added"), sem("msg_ready")
    sems = [idx_loaded, gathers_started, *[a for slot in rows_arrived for a in slot], *attr_arrived, *when_arrived, hot_ready, sums_ready,
            window_added, chain, base_ready, attr_flipped, attr_copied, hid_summed, hid_ready, edge_summed,
            time_summed, gate_ready, gated_ready, msg_summed, msg_added, msg_ready]
    NC = 2 * m.NG
    attr_d = d["attr"].rearrange("(g p j) a -> g p (j a)", p=P, j=TILES)

    def chunk(i, q, lag):
        found = item(i, q, lag, CHUNKS, NC)
        if found is None:
            return None
        c, body, at = found
        k = Names()
        k.c, k.buf, k.first = c, at % 2, at % 2 == 0
        k.group, k.body, k.slot = body * UNROLL + at // 2, body, at // 2
        k.t0, k.t1 = CHUNK_TILES[at % 2]
        k.nt = k.t1 - k.t0
        k.w = k.nt * P
        return k

    def one_pass():
        with nc.Block() as block:
            @block.gpsimd
            def _(pool):
                gather_groups(nc, pool, m, d["y"], idx, rows, idx_loaded, sums_ready, gathers_started, rows_arrived)

            @block.sync
            def _(sp):
                def step(i, q):
                    g = i * UNROLL + q
                    wait_for(sp, attr_flipped, g * 2 - 2 * UNROLL + 2)
                    sp.dma_start(attr[:, q].rearrange("p j a -> p (j a)"),
                                 attr_d[ds(g, 1), :, :].rearrange("o p c -> (o p) c")).then_inc(attr_arrived[q], 16)
                    wait_for(sp, time_summed, g * 2 - 2 * UNROLL + 2)
                    for c in range(3):
                        sp.dma_start(when[3 * c:3 * c + 3, q, :],
                                     d["weight_parts"][c:c + 1, ds(g * GROUP, GROUP)].to_broadcast([3, GROUP])
                                     ).then_inc(when_arrived[q], 16)
                edge_sweep(sp, step, m.NG, UNROLL, 0)

            @block.tensor
            def _(pe):
                def step(i, q):
                    k = chunk(i, q, 0)
                    if k:
                        pe.wait_ge(attr_arrived[k.slot], k.body * 16 + 16)
                        wait_for(pe, attr_copied, k.c)
                    k = chunk(i, q, 1)
                    if k:
                        pe.wait_ge(attr_copied, k.c + 1)
                        wait_for(pe, hid_ready, k.c)
                        nc.tensor.matmul(p_hid[:, 0:k.w], t.We1[:], attrT[:, k.buf, 0:k.w], start=True, stop=True
                                         ).then_inc(hid_summed, 1)
                    k = chunk(i, q, 0)
                    if k:
                        for j in range(k.t0, k.t1):
                            last = nc.tensor.transpose(p_attr[0:A, (j - k.t0) * P:(j - k.t0 + 1) * P], attr[:, k.slot, j, :],
                                                       t.identity[:])
                        last.then_inc(attr_flipped, 1)
                    k = chunk(i, q, 2)
                    if k:
                        pe.wait_ge(when_arrived[k.slot], k.body * 48 + 48)
                        wait_for(pe, gate_ready, k.c)
                        nc.tensor.matmul(p_time[:, 0:k.w].rearrange("f (j p) -> f j p", p=P), t.Wt9[:],
                                         when[:, k.slot, :].rearrange("r (p j) -> r j p", j=TILES)[:, k.t0:k.t1, :],
                                         start=True, stop=True).then_inc(time_summed, 1)
                        pe.wait_ge(hid_ready, k.c + 1)
                        wait_for(pe, gated_ready, k.c)
                        nc.tensor.matmul(p_edge[:, 0:k.w], t.We2[:], hid[:, k.buf, 0:k.w], start=True, stop=True
                                         ).then_inc(edge_summed, 1)
                    k = chunk(i, q, 3)
                    if k:
                        pe.wait_ge(gated_ready, k.c + 1)
                        wait_for(pe, msg_added, k.c)
                        for j in range(k.nt):
                            last = nc.tensor.matmul(p_msg[:, j * P:(j + 1) * P], gated[:, k.buf, j * P:(j + 1) * P], t.Wm_e[:],
                                                    start=True, stop=True)
                        last.then_inc(msg_summed, 1)
                    k = chunk(i, q, 6)
                    if k and k.first:
                        pe.wait_ge(msg_ready, k.c + 2)
                        pe.wait_ge(hot_ready, k.group + 1)
                        wait_for(pe, window_added, k.group if k.slot == 0 else k.group - 1)
                        for j in range(TILES):
                            last = nc.tensor.matmul(win[k.slot % 2][:, 0:WIN], rows[:, k.slot, j, :], hot[:, k.slot, j, :],
                                                    start=j == 0, stop=j == TILES - 1)
                        last.then_inc(sums_ready, 1)
                edge_sweep(pe, step, NC, CHUNKS, 7)

            @block.scalar
            def _(act):
                def step(i, q):
                    k = chunk(i, q, 0)
                    if k and k.first:
                        wait_for(act, msg_added, k.c - 2 * UNROLL + 2)
                        nc.scalar.copy(idx[:, k.slot, :], t.src_idx[:, ds(k.group, 1), :].rearrange("p o j -> p (o j)")
                                       ).then_inc(idx_loaded, 1)
                    if k:
                        act.wait_ge(attr_flipped, k.c + 1)
                        wait_for(act, hid_summed, k.c - 1)
                        nc.scalar.copy(attrT[:, k.buf, 0:k.w], p_attr[0:A, 0:k.w]).then_inc(attr_copied, 1)
                    k = chunk(i, q, 1)
                    if k:
                        act.wait_ge(hid_summed, k.c + 1)
                        wait_for(act, edge_summed, k.c - 1)
                        nc.scalar.activation(hid[:, k.buf, 0:k.w], p_hid[:, 0:k.w], ACT.Relu, bias=t.be1[:, 0:1]
                                             ).then_inc(hid_ready, 1)
                    k = chunk(i, q, 2)
                    if k:
                        act.wait_ge(time_summed, k.c + 1)
                        wait_for(act, gated_ready, k.c - 1)
                        nc.scalar.activation(gate[:, k.buf, 0:k.w], p_time[:, 0:k.w], ACT.Sigmoid, bias=t.bt[:, 0:1]
                                             ).then_inc(gate_ready, 1)
                    k = chunk(i, q, 4)
                    if k:
                        act.wait_ge(msg_added, k.c + 1)
                        nc.scalar.activation(rows[:, k.slot, k.t0:k.t1, :], rows[:, k.slot, k.t0:k.t1, :], ACT.Relu
                                             ).then_inc(msg_ready, 1)
                edge_sweep(act, step, NC, CHUNKS, 4)

            @block.vector
            def _(dve):
                set_windows(nc, dve, m, t, chain, base_ready)

                def step(i, q):
                    k = chunk(i, q, 2)
                    if k:
                        dve.wait_ge(gate_ready, k.c + 1)
                        dve.wait_ge(edge_summed, k.c + 1)
                        wait_for(dve, msg_summed, k.c - 1)
                        nc.vector.scalar_tensor_tensor(gated[:, k.buf, 0:k.w], p_edge[:, 0:k.w], t.be2[:, 0:1],
                                                       gate[:, k.buf, 0:k.w], ALU.add, ALU.mult).then_inc(gated_ready, 1)
                    k = chunk(i, q, 3)
                    if k:
                        for j in range(k.t0, k.t1):
                            dve.wait_ge(rows_arrived[k.slot][j], k.body * 16 + 16)
                        dve.wait_ge(msg_summed, k.c + 1)
                        at = rows[:, k.slot, k.t0:k.t1, :].rearrange("p j f -> p (j f)")
                        nc.vector.tensor_tensor(at, p_msg[:, 0:k.w], at, ALU.add).then_inc(msg_added, 1)
                    k = chunk(i, q, 4)
                    if k and k.first:
                        wait_for(dve, sums_ready, k.group - UNROLL + 1)
                        one_hot(nc, t, hot, k.group, k.slot).then_inc(hot_ready, 1)
                    k = chunk(i, q, 7)
                    if k and k.first:
                        base = dve.value_load(t.base_int[0:1, ds(k.group, 1)], min_val=0, max_val=m.N)
                        wait_for(dve, window_added, k.group)
                        dve.wait_ge(sums_ready, k.group + 1)
                        w = ds(base, WIN)
                        nc.vector.tensor_tensor(t.sums[:, w], t.sums[:, w], win[k.slot % 2][:, 0:WIN],
                                                ALU.add).then_inc(window_added, 1)
                edge_sweep(dve, step, NC, CHUNKS, 8)
        clear_counts(nc, sems, gathered=True)

    all_passes(nc, m, t, one_pass)


def gnn(nc, d):
    m = Names()
    m.N, F = d["x"].shape
    m.E = d["src"].shape[0]
    m.H = d["Ws1"].shape[1]
    m.NG = m.E // GROUP
    m.NB = m.N // BLOCK
    assert F == P and m.NG * GROUP == m.E and m.NG % UNROLL == 0 and m.NB * BLOCK == m.N and m.E % (SUB * GROUP) == 0
    m.WINDOWS = -(-m.N // WIN)
    m.PASS_STRIDE = int(m.WINDOWS ** 0.5)
    d["low"], d["span"] = (nc.dram_tensor(n, [m.NG], FP32).ap() for n in ("group_low", "group_span"))
    d["degree"], d["inv_degree"] = (nc.dram_tensor(n, [m.N], FP32).ap() for n in ("degree_d", "inv_degree_d"))
    d["weight_parts"] = nc.dram_tensor("weight_parts", [3, m.E], BF16).ap()
    d["wt_parts"] = nc.dram_tensor("wt_parts_d", [3, P], BF16).ap()
    d["z"], d["own"], d["x1"], d["y"] = (nc.dram_tensor(n, [m.N, P], FP32).ap() for n in ("z_d", "own_d", "x1_d", "y_d"))

    with ExitStack() as whole:
        def run(tag, build, *args):
            with ExitStack() as part:
                sems = []

                def sem(name):
                    sems.append(part.enter_context(nc.semaphore(tag + name)))
                    return sems[-1]

                build(*args, lambda n, s, dt: part.enter_context(nc.sbuf_tensor(tag + n, s, dt)),
                      lambda n, s, dt: part.enter_context(nc.psum_tensor(tag + n, s, dt)), sem)
                clear_counts(nc, sems)

        def sb(name, shape, dt):
            return whole.enter_context(nc.sbuf_tensor(name, shape, dt))

        t = Names()
        t.rel = sb("rel", [P, m.NG, TILES], FP32)
        t.src_idx = sb("src_idx", [P, m.NG, TILES], I32)
        t.fast_base, t.base_now, t.base_next = (sb(n, [P, m.NG], FP32) for n in ("fast_base", "base_now", "base_next"))
        t.base_int = sb("base_int", [1, m.NG], I32)
        t.passes = sb("passes", [1, 1], I32)
        t.slow_base, t.window_step = sb("slow_base", [P, 1], FP32), sb("window_step", [P, 1], FP32)
        t.identity = sb("identity", [P, P], FP32)
        t.ones, t.ones_row, t.eps = sb("ones", [P, 1], FP32), sb("ones_row", [1, P], FP32), sb("eps", [P, 1], FP32)
        t.We1 = sb("We1", list(d["We1"].shape), FP32)
        t.We2, t.Wm_x, t.Wm_e, t.Wm2 = (sb(n, [P, P], FP32) for n in ("We2", "Wm_x", "Wm_e", "Wm2"))
        t.Ws1, t.Wn1 = sb("Ws1", [P, m.H], FP32), sb("Wn1", [P, m.H], FP32)
        t.Wn2a, t.Ws2a = sb("Wn2a", [P, P], FP32), sb("Ws2a", [P, P], FP32)
        t.Wn2b, t.Ws2b = sb("Wn2b", [m.H - P, P], FP32), sb("Ws2b", [m.H - P, P], FP32)
        t.b1a, t.b1b = sb("b1a", [P, 1], FP32), sb("b1b", [m.H - P, 1], FP32)
        t.be1, t.be2, t.bt = (sb(n, [P, 1], FP32) for n in ("be1", "be2", "bt"))
        t.b2, t.bm1, t.bm2 = (sb(n, [P, P], FP32) for n in ("b2", "bm1", "bm2"))
        t.Wt9 = sb("Wt9", [9, P], BF16)
        t.degree_n, t.inv_n, t.has_n = (sb(n, [SUB, m.NB, NJ], FP32) for n in ("degree_n", "inv_n", "has_n"))
        t.iota_ps = whole.enter_context(nc.psum_tensor("iota_ps", [P, 512], FP32))

        run("load_", load_and_index, nc, m, d, t)
        t.sums = sb("sums", [P, m.N + WIN], FP32)
        with nc.sbuf_tensor("degree", [1, m.N + WIN], FP32) as degree:
            clear_sums(nc, t, [degree[:]])
            run("sum_x_", sum_neighbours, nc, m, t, d["x"], degree)
            run("degree_", invert_degrees, nc, m, d, t, degree)
        run("first_", first_nodes, nc, m, d, t)
        clear_sums(nc, t)
        run("sum_z_", sum_neighbours, nc, m, t, d["z"], None)
        run("second_", second_nodes, nc, m, d, t)
        clear_sums(nc, t)
        run("messages_", sum_messages, nc, m, d, t)
        run("third_", third_nodes, nc, m, d, t)


INPUTS = {
    "x": "x", "src": "src", "dst": "dst", "edge_attr_64": "attr", "edge_weight": "edge_weight",
    "L0_gnn_W_self1": "Ws1", "L0_gnn_W_neigh1": "Wn1", "L0_gnn_b1": "b1",
    "L0_gnn_W_self2": "Ws2", "L0_gnn_W_neigh2": "Wn2", "L0_gnn_b2": "b2",
    "L1_gnn_We1": "We1", "L1_gnn_be1": "be1", "L1_gnn_We2": "We2", "L1_gnn_be2": "be2",
    "L1_gnn_Wt": "Wt", "L1_gnn_bt": "bt", "L1_gnn_Wn1": "Wm1", "L1_gnn_bn1": "bm1",
    "L1_gnn_Wn2": "Wm2", "L1_gnn_bn2": "bm2",
}


def kernel(**inputs):
    import numpy as np
    import concourse.bacc as bacc
    from concourse.bass_utils import run_bass_kernel_spmd

    nc = bacc.Bacc("TRN2", target_bir_lowering=False, num_devices=1)
    arrays, d = {}, {}
    for name, short in INPUTS.items():
        a = np.ascontiguousarray(inputs[name])
        arrays[f"in_{name}"] = a
        ap = nc.dram_tensor(f"in_{name}", a.shape, mybir.dt.from_np(a.dtype), kind="ExternalInput").ap()
        d[short] = ap
    d["out"] = nc.dram_tensor("out", list(inputs["x"].shape), FP32, kind="ExternalOutput").ap()
    gnn(nc, d)
    got = run_bass_kernel_spmd(nc, [arrays], core_ids=[0])
    return got.results[0]["out"]
```

```python
from contextlib import ExitStack

import concourse.bass as bass
from concourse import mybir

FP32 = mybir.dt.float32
BF16 = mybir.dt.bfloat16
I32 = mybir.dt.int32
ALU = mybir.AluOpType
ACT = mybir.ActivationFunctionType
AX = mybir.AxisListType
ds = bass.ds

P = 128
TILES = 5
GROUP = TILES * P
UNROLL = 5
WIN = 64
BLOCK = 500
SUB = 125
NJ = BLOCK // SUB
CHUNKS = 2 * UNROLL
CHUNK_TILES = ((0, 3), (3, 5))
EPS = 1e-5


class Names:
    pass


def wait_for(eng, sem, count):
    if isinstance(count, int) and count < 1:
        return
    eng.wait_ge(sem, count)


def copy_rows(eng, out, in_, sem):
    for a, b in ((0, 112), (112, SUB)):
        eng.dma_start(out[a:b], in_[a:b]).then_inc(sem, 16)


def edge_sweep(eng, step, total, unroll, lag):
    for i in range(2):
        for q in range(unroll):
            step(i, q)
    with eng.Fori(2, total // unroll) as i:
        for q in range(unroll):
            step(i, q)
    for q in range(lag):
        step(total // unroll, q)


def item(i, q, lag, unroll, total):
    if q < lag:
        i, q = i - 1, q + unroll
    n = i * unroll + q - lag
    if isinstance(n, int) and not 0 <= n < total:
        return None
    return n, i, q - lag


def node_sweep(eng, step, total, lag=0):
    peel = 7
    for n in range(peel):
        step(n, n % 2, n // 2)
    with eng.Fori(0, (total - peel) // 2) as i:
        for q in range(2):
            step(i * 2 + (peel + q), (peel + q) % 2, i + (peel + q) // 2)
    for n in range(total, total + lag):
        step(n, n % 2, n // 2)


def block_before(n, slot, turn, lag, total):
    m = n - lag
    if isinstance(m, int):
        return (m, m % 2, m // 2) if 0 <= m < total else None
    if lag % 2 == 0:
        return m, slot, turn - lag // 2
    return m, 1 - slot, turn - (lag + 1) // 2 + slot


def load_and_index(nc, m, d, t, sb, pb, sem):
    rows = m.E // SUB
    dst_i, src_i = sb("dst_i", [SUB, rows], I32), sb("src_i", [SUB, rows], I32)
    dst_f, src_f = dst_i[:].bitcast(FP32), src_i[:].bitcast(FP32)
    rest = sb("rest", [SUB, rows], FP32)
    parts = sb("parts", [SUB, 3, rows], BF16)
    wt_row = sb("wt_row", [1, P], FP32)
    wt_parts = sb("wt_parts", [1, 3, P], BF16)
    groups_row = rows // GROUP
    low = sb("low", [SUB, groups_row], FP32)
    span = sb("span", [SUB, groups_row], FP32)
    span_all = sb("span_all", [P, m.NG], FP32)
    widest = sb("widest", [P, 1], FP32)
    is_slow, is_fast = sb("is_slow", [P, 1], FP32), sb("is_fast", [P, 1], FP32)
    passes_f = sb("passes_f", [1, 1], FP32)
    iota_i, iota_f = sb("iota_i", [1, WIN], I32), sb("iota_f", [1, WIN], FP32)
    FLIPS = 4
    flip = [pb(f"flip{n}", [P, 512], FP32) for n in range(FLIPS)]
    dst_in, src_in, weight_in, params_in = sem("dst_in"), sem("src_in"), sem("weight_in"), sem("params_in")
    identity_ready, iota_ready, ones_ready = sem("identity_ready"), sem("iota_ready"), sem("ones_ready")
    dst_float, src_float, iota_float = sem("dst_float"), sem("src_float"), sem("iota_float")
    low_ready, part_cut, part_taken, wt_ready = sem("low_ready"), sem("part_cut"), sem("part_taken"), sem("wt_ready")
    low_stored, parts_stored, wt_stored = sem("low_stored"), sem("parts_stored"), sem("wt_stored")
    low_back, wt_back = sem("low_back"), sem("wt_back")
    flipped, even_copied, odd_copied = sem("flipped"), sem("even_copied"), sem("odd_copied")
    chain, pool_chain, iota_spread = sem("chain"), sem("pool_chain"), sem("iota_spread")

    flips = [(src, out, k, j) for src, out in ((src_f, t.src_idx), (dst_f, t.rel))
             for k in range(groups_row) for j in range(TILES)]

    def take_flip(copy, n):
        _, out, k, j = flips[n]
        return copy(out[:].rearrange("p (q k) j -> p q k j", k=groups_row)[:, :, k, j], flip[n % FLIPS][:, 0:SUB])

    with nc.Block() as block:
        @block.sync
        def _(sp):
            copy_rows(sp, src_i, d["src"].rearrange("(q r) -> q r", q=SUB), src_in)
            copy_rows(sp, dst_i, d["dst"].rearrange("(q r) -> q r", q=SUB), dst_in)
            copy_rows(sp, rest, d["edge_weight"].rearrange("(q r) -> q r", q=SUB), weight_in)
            sp.dma_start(wt_row[:], d["Wt"]).then_inc(weight_in, 16)
            sp.wait_ge(low_ready, 1)
            sp.dma_start(d["low"].rearrange("(q k) -> q k", q=SUB), low[:]).then_inc(low_stored, 16)
            sp.dma_start(d["span"].rearrange("(q k) -> q k", q=SUB), span[:]).then_inc(low_stored, 16)
            sp.wait_ge(low_stored, 32)
            sp.dma_start(t.fast_base[:], d["low"].partition_broadcast(P)).then_inc(low_back, 16)
            sp.dma_start(span_all[:], d["span"].partition_broadcast(P)).then_inc(low_back, 16)
            sp.wait_ge(wt_ready, 1)
            sp.dma_start(d["wt_parts"].rearrange("(o c) f -> o c f", o=1), wt_parts[:]).then_inc(wt_stored, 16)
            sp.wait_ge(wt_stored, 16)
            for c in range(3):
                sp.dma_start(t.Wt9[3 * c:3 * c + 3, :], d["wt_parts"]).then_inc(wt_back, 16)
            for c in range(3):
                sp.wait_ge(part_cut, c + 1)
                copy_rows(sp, d["weight_parts"][c, :].rearrange("(q r) -> q r", q=SUB), parts[:, c, :], parts_stored)
            sp.wait_ge(wt_back, 48)
            sp.wait_ge(low_back, 32)
            sp.wait_ge(parts_stored, 96)

        @block.scalar
        def _(act):
            act.wait_ge(src_in, 32)
            nc.scalar.copy(src_f, src_i[:]).then_inc(src_float, 1)
            loads = [
                (t.We1[:], d["We1"]), (t.We2[:], d["We2"]), (t.Wm_x[:], d["Wm1"][0:P, :]), (t.Wm_e[:], d["Wm1"][P:2 * P, :]),
                (t.Wm2[:], d["Wm2"]), (t.Ws1[:], d["Ws1"]), (t.Wn1[:], d["Wn1"]),
                (t.Wn2a[:], d["Wn2"][0:P, :]), (t.Wn2b[:], d["Wn2"][P:m.H, :]),
                (t.Ws2a[:], d["Ws2"][0:P, :]), (t.Ws2b[:], d["Ws2"][P:m.H, :]),
                (t.b1a[:], d["b1"][0:P].rearrange("(f o) -> f o", o=1)), (t.b1b[:], d["b1"][P:m.H].rearrange("(f o) -> f o", o=1)),
                (t.be1[:], d["be1"].rearrange("(f o) -> f o", o=1)), (t.be2[:], d["be2"].rearrange("(f o) -> f o", o=1)),
                (t.bt[:], d["bt"].rearrange("(f o) -> f o", o=1)),
                (t.b2[:], d["b2"].partition_broadcast(P)), (t.bm1[:], d["bm1"].partition_broadcast(P)),
                (t.bm2[:], d["bm2"].partition_broadcast(P)),
            ]
            for out, in_ in loads:
                act.dma_start(out, in_).then_inc(params_in, 16)
            for n in range(0, len(flips), 2):
                act.wait_ge(flipped, n + 1)
                take_flip(nc.scalar.copy, n).then_inc(even_copied, 1)
            act.wait_ge(weight_in, 48)
            for c in range(3):
                if c > 0:
                    act.wait_ge(part_taken, c)
                nc.scalar.copy(parts[:, c, :], rest[:]).then_inc(part_cut, 1)
            act.wait_ge(params_in, 16 * len(loads))

        @block.gpsimd
        def _(pool):
            nc.gpsimd.memset(t.identity[:], 0.0).then_inc(pool_chain, 1)
            pool.wait_ge(pool_chain, 1)
            nc.gpsimd.affine_select(out=t.identity[:], in_=t.identity[:], compare_op=ALU.not_equal, fill=1.0,
                                    base=0, pattern=[[-1, P]], channel_multiplier=1).then_inc(identity_ready, 1)
            nc.gpsimd.iota(iota_i[:], pattern=[[1, WIN]], base=0, channel_multiplier=0).then_inc(iota_ready, 1)
            nc.gpsimd.memset(t.ones[:], 1.0).then_inc(ones_ready, 1)
            nc.gpsimd.memset(t.ones_row[:], 1.0).then_inc(ones_ready, 1)
            nc.gpsimd.memset(t.eps[:], EPS).then_inc(ones_ready, 1)
            nc.gpsimd.memset(t.zeros[:], 0.0).then_inc(ones_ready, 1)
            nc.gpsimd.memset(t.sums[:], 0.0).then_inc(ones_ready, 1)

        @block.vector
        def _(dve):
            done = [0]

            def then(ins):
                done[0] += 1
                ins.then_inc(chain, 1)
                dve.wait_ge(chain, done[0])

            dve.wait_ge(iota_ready, 1)
            nc.vector.tensor_copy(iota_f[:], iota_i[:]).then_inc(iota_float, 1)
            for n in range(1, len(flips) // 2, 2):
                dve.wait_ge(flipped, n + 1)
                take_flip(nc.vector.tensor_copy, n).then_inc(odd_copied, 1)
            dve.wait_ge(dst_in, 32)
            nc.vector.tensor_copy(dst_f, dst_i[:]).then_inc(dst_float, 1)
            dve.wait_ge(dst_float, 1)
            by_group = dst_f.rearrange("q (k e) -> q k e", e=GROUP)
            then(nc.vector.tensor_reduce(low[:], by_group, axis=AX.X, op=ALU.min))
            then(nc.vector.tensor_reduce(span[:], by_group, axis=AX.X, op=ALU.max))
            nc.vector.tensor_tensor(span[:], span[:], low[:], ALU.subtract).then_inc(low_ready, 1)
            for n in range(len(flips) // 2 + (len(flips) // 2 + 1) % 2, len(flips), 2):
                dve.wait_ge(flipped, n + 1)
                take_flip(nc.vector.tensor_copy, n).then_inc(odd_copied, 1)
            dve.wait_ge(weight_in, 48)
            then(nc.vector.tensor_copy(wt_parts[:, 0, :], wt_row[:]))
            then(nc.vector.tensor_tensor(wt_row[:], wt_row[:], wt_parts[:, 0, :], ALU.subtract))
            then(nc.vector.tensor_copy(wt_parts[:, 1, :], wt_row[:]))
            then(nc.vector.tensor_tensor(wt_row[:], wt_row[:], wt_parts[:, 1, :], ALU.subtract))
            nc.vector.tensor_copy(wt_parts[:, 2, :], wt_row[:]).then_inc(wt_ready, 1)
            for c in range(2):
                dve.wait_ge(part_cut, c + 1)
                nc.vector.tensor_tensor(rest[:], rest[:], parts[:, c, :], ALU.subtract).then_inc(part_taken, 1)
            dve.wait_ge(low_back, 32)
            then(nc.vector.tensor_reduce(widest[:], span_all[:], axis=AX.X, op=ALU.max))
            then(nc.vector.tensor_scalar(is_slow[:], widest[:], float(WIN), None, ALU.is_ge))
            then(nc.vector.tensor_scalar(is_fast[:], widest[:], float(WIN), None, ALU.is_lt))
            then(nc.vector.tensor_scalar(t.window_step[:], is_slow[:], float(WIN), None, ALU.mult))
            then(nc.vector.tensor_scalar(t.fast_base[:], t.fast_base[:], is_fast[:, 0:1], None, ALU.mult))
            then(nc.vector.tensor_scalar(passes_f[:], is_slow[0:1, :], float(m.WINDOWS - 1), 1.0, ALU.mult, ALU.add))
            then(nc.vector.tensor_copy(t.passes[:], passes_f[:]))
            then(nc.vector.memset(t.base_now[:], 0.0))
            then(nc.vector.memset(t.slow_base[:], 0.0))

        @block.tensor
        def _(pe):
            pe.wait_ge(ones_ready, 2)
            pe.wait_ge(iota_float, 1)
            nc.tensor.matmul(t.iota_ps[:, 0:WIN], t.ones_row[:], iota_f[:], start=True, stop=True).then_inc(iota_spread, 1)
            pe.wait_ge(identity_ready, 1)
            pe.wait_ge(src_float, 1)
            for n, (source, _, k, j) in enumerate(flips):
                if n == len(flips) // 2:
                    pe.wait_ge(dst_float, 1)
                if n >= FLIPS:
                    pe.wait_ge(odd_copied if n % 2 else even_copied, (n - FLIPS) // 2 + 1)
                nc.tensor.transpose(flip[n % FLIPS][:, 0:SUB],
                                    source.rearrange("q (k p j) -> q k j p", p=P, j=TILES)[:, k, j, :],
                                    t.identity[0:SUB, 0:SUB]).then_inc(flipped, 1)
            pe.wait_ge(iota_spread, 1)


def set_windows(nc, dve, m, t, chain, base_ready):
    done = [0]

    def then(ins):
        done[0] += 1
        ins.then_inc(chain, 1)
        dve.wait_ge(chain, done[0])

    then(nc.vector.tensor_scalar(t.base_next[:], t.fast_base[:], t.slow_base[:, 0:1], None, ALU.add))
    then(nc.vector.tensor_tensor(t.base_now[:], t.base_now[:], t.base_next[:], ALU.subtract))
    then(nc.vector.tensor_tensor(t.rel[:], t.rel[:], t.base_now[:].unsqueeze(2).to_broadcast([P, m.NG, TILES]), ALU.add))
    then(nc.vector.tensor_copy(t.base_now[:], t.base_next[:]))
    then(nc.vector.tensor_tensor(t.slow_base[:], t.slow_base[:], t.window_step[:], ALU.add))
    nc.vector.tensor_copy(t.base_int[:], t.base_next[0:1, :]).then_inc(base_ready, 1)
    dve.wait_ge(base_ready, 1)


def one_hot(nc, t, hot, g, slot):
    return nc.vector.tensor_tensor(
        hot[:, slot],
        t.iota_ps[:, 0:WIN].unsqueeze(1).to_broadcast([P, TILES, WIN]),
        t.rel[:, ds(g, 1), :].rearrange("p o j -> p (o j)").unsqueeze(2).to_broadcast([P, TILES, WIN]), ALU.is_equal)


def gather_groups(nc, pool, m, table, idx, rows, idx_loaded, sums_ready, gathers_started, rows_arrived):
    def step(i, q):
        g = i * UNROLL + q
        wait_for(pool, sums_ready, g - UNROLL + 1)
        pool.wait_ge(idx_loaded, g + 1)
        pool.sem_inc(gathers_started, 1)
        for j in range(TILES):
            nc.gpsimd.indirect_dma_start(
                out=rows[:, q, j, :], out_offset=None, in_=table,
                in_offset=bass.IndirectOffsetOnAxis(ap=idx[:, q, j:j + 1], axis=0)).then_inc(rows_arrived[q][j], 16)
    edge_sweep(pool, step, m.NG, UNROLL, 0)
    for slot in rows_arrived:
        for tile_arrived in slot:
            pool.wait_ge(tile_arrived, m.NG // UNROLL * 16)


def clear_counts(nc, sems, gathered=False):
    if gathered:
        nc.gpsimd.dma_reset()
    for s in sems:
        nc.gpsimd.sem_clear(s)
    nc.all_engine_barrier()


def sum_neighbours(nc, m, t, table, degree, sb, pb, sem):
    idx = sb("idx", [P, UNROLL, TILES], I32)
    rows = sb("rows", [P, UNROLL, TILES, P], FP32)
    hot = sb("hot", [P, UNROLL, TILES, WIN], FP32)
    bank = (0, 1, 0, 1, 2)
    win = [pb(f"win{b}", [P, 512], FP32) for b in range(3)]
    cnt = [pb(f"cnt{b}", [P, 512], FP32) for b in range(3)] if degree is not None else []
    idx_loaded, gathers_started = sem("idx_loaded"), sem("gathers_started")
    rows_arrived = [[sem(f"rows_arrived{q}_{j}") for j in range(TILES)] for q in range(UNROLL)]
    hot_ready, sums_ready, window_added = sem("hot_ready"), sem("sums_ready"), sem("window_added")
    chain, base_ready = sem("chain"), sem("base_ready")
    sems = [idx_loaded, gathers_started, *[a for slot in rows_arrived for a in slot], hot_ready, sums_ready, window_added, chain, base_ready]

    def one_pass():
        with nc.Block() as block:
            @block.gpsimd
            def _(pool):
                gather_groups(nc, pool, m, table, idx, rows, idx_loaded, sums_ready, gathers_started, rows_arrived)

            @block.scalar
            def _(act):
                def step(i, q):
                    g = i * UNROLL + q
                    wait_for(act, sums_ready, g - UNROLL + 1)
                    nc.scalar.copy(idx[:, q, :], t.src_idx[:, ds(g, 1), :].rearrange("p o j -> p (o j)")).then_inc(idx_loaded, 1)
                edge_sweep(act, step, m.NG, UNROLL, 0)

            @block.vector
            def _(dve):
                set_windows(nc, dve, m, t, chain, base_ready)

                def step(i, q):
                    now = item(i, q, 0, UNROLL, m.NG)
                    if now:
                        g, _, slot = now
                        wait_for(dve, sums_ready, g - UNROLL + 1)
                        one_hot(nc, t, hot, g, slot).then_inc(hot_ready, 1)
                    late = item(i, q, 2, UNROLL, m.NG)
                    if late:
                        g, _, slot = late
                        base = dve.value_load(t.base_int[0:1, ds(g, 1)], min_val=0, max_val=m.N)
                        wait_for(dve, window_added, g)
                        dve.wait_ge(sums_ready, g + 1)
                        w = ds(base, WIN)
                        if degree is not None:
                            nc.vector.tensor_tensor(degree[:, w], degree[:, w], cnt[bank[slot]][0:1, 0:WIN], ALU.add)
                        nc.vector.tensor_tensor(t.sums[:, w], t.sums[:, w], win[bank[slot]][:, 0:WIN],
                                                ALU.add).then_inc(window_added, 1)
                edge_sweep(dve, step, m.NG, UNROLL, 2)

            @block.tensor
            def _(pe):
                def step(i, q):
                    g = i * UNROLL + q
                    wait_for(pe, window_added, g - 1)
                    pe.wait_ge(hot_ready, g + 1)
                    for j in range(TILES):
                        pe.wait_ge(rows_arrived[q][j], i * 16 + 16)
                    for j in range(TILES):
                        last = nc.tensor.matmul(win[bank[q]][:, 0:WIN], rows[:, q, j, :], hot[:, q, j, :],
                                                start=j == 0, stop=j == TILES - 1)
                    if degree is not None:
                        for j in range(TILES):
                            last = nc.tensor.matmul(cnt[bank[q]][0:1, 0:WIN], t.ones[:], hot[:, q, j, :],
                                                    start=j == 0, stop=j == TILES - 1)
                    last.then_inc(sums_ready, 1)
                edge_sweep(pe, step, m.NG, UNROLL, 0)

            @block.sync
            def _(sp):
                sp.wait_ge(window_added, m.NG)
        clear_counts(nc, sems, gathered=True)

    all_passes(nc, m, t, one_pass)


def all_passes(nc, m, t, one_pass):
    passes = nc.values_load(t.passes[0:1, 0:1], min_val=1, max_val=m.WINDOWS)
    fine = -(-round(m.WINDOWS ** (1 / 3) * 100) // 100)
    with nc.Fori(0, m.WINDOWS, fine * fine) as outer:
        with nc.If(outer < passes):
            with nc.Fori(0, fine * fine, fine) as middle:
                with nc.If(outer + middle < passes):
                    with nc.Fori(0, fine) as inner:
                        with nc.If(outer + middle + inner < passes):
                            one_pass()


def clear_block(nc, act, t, mean_ready, n):
    act.wait_ge(mean_ready, n + 1)
    nc.scalar.copy(t.sums[:, ds(n * BLOCK, BLOCK)], t.zeros[:])


def mean_block(nc, pool, t, mean, inv, n, slot):
    return nc.gpsimd.tensor_tensor(mean[:, slot], t.sums[:, ds(n * BLOCK, BLOCK)].rearrange("f (p j) -> f j p", j=NJ),
                                   inv[:, slot].rearrange("f (p j) -> f j p", j=NJ), ALU.mult)


def node_rows(ap, n):
    return ap.rearrange("(b p j) f -> b p (j f)", p=SUB, j=NJ)[ds(n, 1), :, :].rearrange("o p c -> (o p) c")


def invert_degrees(nc, m, d, t, degree, sb, pb, sem):
    stored, back, inv_ready, inv_stored, chain = sem("stored"), sem("back"), sem("inv_ready"), sem("inv_stored"), sem("chain")
    with nc.Block() as block:
        @block.sync
        def _(sp):
            sp.dma_start(d["degree"].rearrange("(o n) -> o n", o=1), degree[:, 0:m.N]).then_inc(stored, 16)
            sp.wait_ge(stored, 16)
            sp.dma_start(t.degree_n[:], d["degree"].rearrange("(b p j) -> p b j", p=SUB, j=NJ)).then_inc(back, 16)
            sp.wait_ge(inv_ready, 1)
            sp.dma_start(d["inv_degree"].rearrange("(b p j) -> p b j", p=SUB, j=NJ), t.inv_n[:]).then_inc(inv_stored, 16)
            sp.wait_ge(inv_stored, 16)

        @block.vector
        def _(dve):
            done = [0]

            def then(ins):
                done[0] += 1
                ins.then_inc(chain, 1)
                dve.wait_ge(chain, done[0])

            dve.wait_ge(back, 16)
            then(nc.vector.tensor_scalar(t.inv_n[:], t.degree_n[:], 1.0, None, ALU.max))
            then(nc.vector.reciprocal(t.inv_n[:], t.inv_n[:]))
            then(nc.vector.tensor_scalar(t.has_n[:], t.degree_n[:], 0.0, None, ALU.is_gt))
            nc.vector.tensor_tensor(t.inv_n[:], t.inv_n[:], t.has_n[:], ALU.mult).then_inc(inv_ready, 1)


def first_nodes(nc, m, d, t, sb, pb, sem):
    x = sb("x", [SUB, 2, NJ * P], FP32)
    inv = sb("inv", [P, 2, BLOCK], FP32)
    mean = sb("mean", [P, 2, NJ, SUB], FP32)
    xb = sb("xb", [SUB, 2, NJ, P], FP32)
    xT = sb("xT", [P, 2, BLOCK], FP32)
    hA, hB = sb("hA", [P, 2, NJ, SUB], FP32), sb("hB", [m.H - P, 2, NJ, SUB], FP32)
    z, own = sb("z", [SUB, 2, NJ * P], FP32), sb("own", [SUB, 2, NJ * P], FP32)
    p_x, p_hA, p_hB = pb("p_x", [P, 512], FP32), pb("p_hA", [P, 512], FP32), pb("p_hB", [P, 512], FP32)
    p_z, p_own = pb("p_z", [P, 512], FP32), pb("p_own", [P, 512], FP32)
    x_in, inv_in = [sem("x_in0"), sem("x_in1")], [sem("inv_in0"), sem("inv_in1")]
    z_out, own_out = [sem("z_out0"), sem("z_out1")], [sem("own_out0"), sem("own_out1")]
    mean_ready, xb_ready, x_flipped, x_copied = sem("mean_ready"), sem("xb_ready"), sem("x_flipped"), sem("x_copied")
    h_summed, h_ready, out_summed = sem("h_summed"), sem("h_ready"), sem("out_summed")
    z_ready, own_ready = sem("z_ready"), sem("own_ready")

    with nc.Block() as block:
        @block.sync
        def _(sp):
            def step(n, slot, turn):
                now = block_before(n, slot, turn, 0, m.NB)
                if now:
                    wait_for(sp, x_flipped, n - 1)
                    wait_for(sp, xb_ready, n - 1)
                    wait_for(sp, mean_ready, n - 1)
                    copy_rows(sp, x[:, slot], node_rows(d["x"], n), x_in[slot])
                    sp.dma_start(inv[:, slot], d["inv_degree"][ds(n * BLOCK, BLOCK)].partition_broadcast(P)).then_inc(inv_in[slot], 16)
                late = block_before(n, slot, turn, 3, m.NB)
                if late:
                    n, slot, turn = late
                    sp.wait_ge(z_ready, n + 1)
                    copy_rows(sp, node_rows(d["z"], n), z[:, slot], z_out[slot])
                    sp.wait_ge(own_ready, n + 1)
                    copy_rows(sp, node_rows(d["own"], n), own[:, slot], own_out[slot])
            node_sweep(sp, step, m.NB, 3)
            for slot in range(2):
                uses = (m.NB + 1 - slot) // 2
                sp.wait_ge(z_out[slot], 32 * uses)
                sp.wait_ge(own_out[slot], 32 * uses)

        @block.gpsimd
        def _(pool):
            def step(n, slot, turn):
                pool.wait_ge(inv_in[slot], turn * 16 + 16)
                wait_for(pool, h_summed, n - 1)
                mean_block(nc, pool, t, mean, inv, n, slot).then_inc(mean_ready, 1)
                pool.wait_ge(x_in[slot], turn * 32 + 32)
                wait_for(pool, own_ready, n - 1)
                nc.gpsimd.tensor_tensor(xb[:, slot], x[:, slot].rearrange("p (j f) -> p j f", j=NJ),
                                        t.b2[0:SUB, :].unsqueeze(1).to_broadcast([SUB, NJ, P]), ALU.add).then_inc(xb_ready, 1)
            node_sweep(pool, step, m.NB)

        @block.tensor
        def _(pe):
            def step(n, slot, turn):
                now = block_before(n, slot, turn, 0, m.NB)
                if now:
                    b, s, use = now
                    pe.wait_ge(x_in[s], use * 32 + 32)
                    wait_for(pe, x_copied, b)
                    for j in range(NJ):
                        last = nc.tensor.transpose(p_x[:, j * SUB:(j + 1) * SUB], x[:, s, j * P:(j + 1) * P],
                                                   t.identity[0:SUB, 0:SUB])
                    last.then_inc(x_flipped, 1)
                mid = block_before(n, slot, turn, 1, m.NB)
                if mid:
                    b, s, _ = mid
                    pe.wait_ge(x_copied, b + 1)
                    pe.wait_ge(mean_ready, b + 1)
                    wait_for(pe, h_ready, b)
                    for bank, k0, k1 in ((p_hA, 0, P), (p_hB, P, m.H)):
                        out = bank[0:k1 - k0, 0:BLOCK]
                        nc.tensor.matmul(out, t.Ws1[:, k0:k1], xT[:, s, :], start=True, stop=False)
                        last = nc.tensor.matmul(out, t.Wn1[:, k0:k1], mean[:, s].rearrange("f j p -> f (j p)"),
                                                start=False, stop=True)
                    last.then_inc(h_summed, 1)
                late = block_before(n, slot, turn, 2, m.NB)
                if late:
                    b, s, _ = late
                    pe.wait_ge(h_ready, b + 1)
                    wait_for(pe, z_ready, b)
                    wait_for(pe, own_ready, b)
                    for bank, wa, wb in ((p_z, t.Wn2a, t.Wn2b), (p_own, t.Ws2a, t.Ws2b)):
                        for j in range(NJ):
                            out = bank[0:SUB, j * P:(j + 1) * P]
                            nc.tensor.matmul(out, hA[:, s, j, :], wa[:], start=True, stop=False)
                            last = nc.tensor.matmul(out, hB[:, s, j, :], wb[:], start=False, stop=True)
                    last.then_inc(out_summed, 1)
            node_sweep(pe, step, m.NB, 2)

        @block.scalar
        def _(act):
            def step(n, slot, turn):
                now = block_before(n, slot, turn, 0, m.NB)
                if now:
                    b, s, _ = now
                    act.wait_ge(x_flipped, b + 1)
                    wait_for(act, h_summed, b - 1)
                    nc.scalar.copy(xT[:, s, :], p_x[:, 0:BLOCK]).then_inc(x_copied, 1)
                mid = block_before(n, slot, turn, 1, m.NB)
                if mid:
                    b, s, _ = mid
                    act.wait_ge(h_summed, b + 1)
                    wait_for(act, out_summed, b - 1)
                    nc.scalar.activation(hA[:, s].rearrange("f j p -> f (j p)"), p_hA[:, 0:BLOCK], ACT.Relu, bias=t.b1a[:, 0:1])
                    nc.scalar.activation(hB[:, s].rearrange("f j p -> f (j p)"), p_hB[0:m.H - P, 0:BLOCK], ACT.Relu,
                                         bias=t.b1b[:, 0:1]).then_inc(h_ready, 1)
                late = block_before(n, slot, turn, 2, m.NB)
                if late:
                    b, s, use = late
                    act.wait_ge(out_summed, b + 1)
                    wait_for(act, z_out[s], use * 32)
                    nc.scalar.copy(z[:, s, :], p_z[0:SUB, :]).then_inc(z_ready, 1)
                    clear_block(nc, act, t, mean_ready, b)
            node_sweep(act, step, m.NB, 2)

        @block.vector
        def _(dve):
            nc.vector.memset(t.slow_base[:], 0.0)

            def step(n, slot, turn):
                late = block_before(n, slot, turn, 2, m.NB)
                if late:
                    b, s, use = late
                    dve.wait_ge(out_summed, b + 1)
                    dve.wait_ge(xb_ready, b + 1)
                    wait_for(dve, own_out[s], use * 32)
                    nc.vector.tensor_tensor(own[:, s, :], p_own[0:SUB, :], xb[:, s].rearrange("p j f -> p (j f)"),
                                            ALU.add).then_inc(own_ready, 1)
            node_sweep(dve, step, m.NB, 2)


def norm_buffers(sb, sem):
    k = Names()
    k.u, k.normed = sb("u", [SUB, 2, NJ, P], FP32), sb("normed", [SUB, 2, NJ, P], FP32)
    k.stats, k.moments = sb("stats", [SUB, 2, NJ, 6], FP32), sb("moments", [SUB, 2, NJ, 2], FP32)
    k.std, k.scale = sb("std", [SUB, 2, NJ], FP32), sb("scale", [SUB, 2, NJ], FP32)
    k.u_ready, k.stats_ready, k.aggregates_started = sem("u_ready"), sem("stats_ready"), sem("aggregates_started")
    k.moments_ready, k.std_ready, k.scale_ready = sem("moments_ready"), sem("std_ready"), sem("scale_ready")
    k.normed_ready = sem("normed_ready")
    return k


def norm_moments(nc, dve, k, b, s):
    dve.wait_ge(k.u_ready, b + 1)
    for j in range(NJ):
        last = nc.vector.bn_stats(k.stats[:, s, j, :], k.u[:, s, j, :])
    last.then_inc(k.stats_ready, 1)
    dve.wait_ge(k.stats_ready, b + 1)
    dve.sem_inc(k.aggregates_started, 1)
    for j in range(NJ):
        last = nc.vector.bn_aggr(k.moments[:, s, j, :], k.stats[:, s, j, :])
    last.then_inc(k.moments_ready, 1)


def norm_std(nc, act, t, k, b, s):
    act.wait_ge(k.moments_ready, b + 1)
    nc.scalar.activation(k.std[:, s, :], k.moments[:, s, :, 1], ACT.Sqrt, bias=t.eps[0:SUB, 0:1]).then_inc(k.std_ready, 1)


def norm_apply(nc, dve, k, b, s):
    dve.wait_ge(k.std_ready, b + 1)
    nc.vector.reciprocal(k.scale[:, s, :], k.std[:, s, :]).then_inc(k.scale_ready, 1)
    dve.wait_ge(k.scale_ready, b + 1)
    for j in range(NJ):
        last = nc.vector.tensor_scalar(k.normed[:, s, j, :], k.u[:, s, j, :], k.moments[:, s, j, 0:1],
                                       k.scale[:, s, j:j + 1], ALU.subtract, ALU.mult)
    last.then_inc(k.normed_ready, 1)


def second_nodes(nc, m, d, t, sb, pb, sem):
    own = sb("own", [SUB, 2, NJ * P], FP32)
    inv = sb("inv", [P, 2, BLOCK], FP32)
    mean = sb("mean", [P, 2, NJ, SUB], FP32)
    x1T = sb("x1T", [P, 2, NJ, SUB], FP32)
    y = sb("y", [SUB, 2, NJ, P], FP32)
    twice = sb("twice", [SUB, 2, NJ, P], FP32)
    bias = sb("bias", [SUB, 2, NJ, P], FP32)
    base = sb("base", [SUB, 2, NJ, P], FP32)
    p_mean, p_x1, p_y = pb("p_mean", [P, 512], FP32), pb("p_x1", [P, 512], FP32), pb("p_y", [P, 512], FP32)
    k = norm_buffers(sb, sem)
    own_in, inv_in = [sem("own_in0"), sem("own_in1")], [sem("inv_in0"), sem("inv_in1")]
    base_out, y_out = [sem("base_out0"), sem("base_out1")], [sem("y_out0"), sem("y_out1")]
    mean_ready, mean_flipped, x1_flipped, x1_copied = sem("mean_ready"), sem("mean_flipped"), sem("x1_flipped"), sem("x1_copied")
    y_summed, y_ready = sem("y_summed"), sem("y_ready")
    twice_ready, bias_ready, base_ready = sem("twice_ready"), sem("bias_ready"), sem("base_ready")

    with nc.Block() as block:
        @block.sync
        def _(sp):
            def step(n, slot, turn):
                now = block_before(n, slot, turn, 0, m.NB)
                if now:
                    wait_for(sp, k.u_ready, n - 1)
                    wait_for(sp, mean_ready, n - 1)
                    copy_rows(sp, own[:, slot], node_rows(d["own"], n), own_in[slot])
                    sp.dma_start(inv[:, slot], d["inv_degree"][ds(n * BLOCK, BLOCK)].partition_broadcast(P)).then_inc(inv_in[slot], 16)
                late = block_before(n, slot, turn, 4, m.NB)
                if late:
                    b, s, _ = late
                    sp.wait_ge(base_ready, b + 1)
                    copy_rows(sp, node_rows(d["base"], b), base[:, s].rearrange("p j f -> p (j f)"), base_out[s])
                last = block_before(n, slot, turn, 5, m.NB)
                if last:
                    b, s, _ = last
                    sp.wait_ge(y_ready, b + 1)
                    copy_rows(sp, node_rows(d["y"], b), y[:, s].rearrange("p j f -> p (j f)"), y_out[s])
            node_sweep(sp, step, m.NB, 5)
            for slot in range(2):
                uses = (m.NB + 1 - slot) // 2
                sp.wait_ge(base_out[slot], 32 * uses)
                sp.wait_ge(y_out[slot], 32 * uses)

        @block.gpsimd
        def _(pool):
            def step(n, slot, turn):
                now = block_before(n, slot, turn, 0, m.NB)
                if now:
                    b, s, use = now
                    pool.wait_ge(inv_in[s], use * 16 + 16)
                    wait_for(pool, mean_flipped, b - 1)
                    mean_block(nc, pool, t, mean, inv, b, s).then_inc(mean_ready, 1)
                late = block_before(n, slot, turn, 3, m.NB)
                if late:
                    b, s, use = late
                    wait_for(pool, base_ready, b - 1)
                    nc.gpsimd.tensor_tensor(bias[:, s], t.bm2[0:SUB, :].unsqueeze(1).to_broadcast([SUB, NJ, P]),
                                            t.degree_n[:, ds(b, 1), :].rearrange("p o j -> p (o j)").unsqueeze(2).to_broadcast([SUB, NJ, P]),
                                            ALU.mult).then_inc(bias_ready, 1)
                    pool.wait_ge(twice_ready, b + 1)
                    pool.wait_ge(bias_ready, b + 1)
                    wait_for(pool, base_out[s], use * 32)
                    nc.gpsimd.tensor_tensor(base[:, s], twice[:, s], bias[:, s], ALU.add).then_inc(base_ready, 1)
            node_sweep(pool, step, m.NB, 3)

        @block.tensor
        def _(pe):
            def step(n, slot, turn):
                now = block_before(n, slot, turn, 0, m.NB)
                if now:
                    b, s, _ = now
                    pe.wait_ge(mean_ready, b + 1)
                    wait_for(pe, k.u_ready, b)
                    for j in range(NJ):
                        last = nc.tensor.transpose(p_mean[0:SUB, j * P:(j + 1) * P], mean[:, s, j, :], t.identity[:])
                    last.then_inc(mean_flipped, 1)
                mid = block_before(n, slot, turn, 2, m.NB)
                if mid:
                    b, s, _ = mid
                    pe.wait_ge(k.normed_ready, b + 1)
                    wait_for(pe, x1_copied, b)
                    for j in range(NJ):
                        last = nc.tensor.transpose(p_x1[:, j * SUB:(j + 1) * SUB], k.normed[:, s, j, :],
                                                   t.identity[0:SUB, 0:SUB])
                    last.then_inc(x1_flipped, 1)
                late = block_before(n, slot, turn, 3, m.NB)
                if late:
                    b, s, _ = late
                    pe.wait_ge(x1_copied, b + 1)
                    wait_for(pe, y_ready, b)
                    for j in range(NJ):
                        last = nc.tensor.matmul(p_y[0:SUB, j * P:(j + 1) * P], x1T[:, s, j, :], t.Wm_x[:],
                                                start=True, stop=True)
                    last.then_inc(y_summed, 1)
            node_sweep(pe, step, m.NB, 3)

        @block.scalar
        def _(act):
            def step(n, slot, turn):
                now = block_before(n, slot, turn, 0, m.NB)
                if now:
                    norm_std(nc, act, t, k, now[0], now[1])
                    clear_block(nc, act, t, mean_ready, now[0])
                mid = block_before(n, slot, turn, 2, m.NB)
                if mid:
                    b, s, _ = mid
                    act.wait_ge(k.normed_ready, b + 1)
                    wait_for(act, base_ready, b - 1)
                    nc.scalar.mul(twice[:, s], k.normed[:, s], 2.0).then_inc(twice_ready, 1)
                    act.wait_ge(x1_flipped, b + 1)
                    wait_for(act, y_summed, b - 1)
                    nc.scalar.copy(x1T[:, s].rearrange("f j p -> f (j p)"), p_x1[:, 0:BLOCK]).then_inc(x1_copied, 1)
            node_sweep(act, step, m.NB, 2)

        @block.vector
        def _(dve):
            nc.vector.memset(t.slow_base[:], 0.0)

            def step(n, slot, turn):
                now = block_before(n, slot, turn, 0, m.NB)
                if now:
                    b, s, use = now
                    dve.wait_ge(own_in[s], use * 32 + 32)
                    dve.wait_ge(mean_flipped, b + 1)
                    wait_for(dve, k.normed_ready, b - 1)
                    nc.vector.tensor_tensor(k.u[:, s].rearrange("p j f -> p (j f)"), p_mean[0:SUB, :], own[:, s, :],
                                            ALU.add).then_inc(k.u_ready, 1)
                    norm_moments(nc, dve, k, b, s)
                mid = block_before(n, slot, turn, 1, m.NB)
                if mid:
                    b, s, use = mid
                    wait_for(dve, twice_ready, b - 1)
                    wait_for(dve, x1_flipped, b - 1)
                    norm_apply(nc, dve, k, b, s)
                late = block_before(n, slot, turn, 4, m.NB)
                if late:
                    b, s, use = late
                    dve.wait_ge(y_summed, b + 1)
                    wait_for(dve, y_out[s], use * 32)
                    nc.vector.tensor_tensor(y[:, s], p_y[0:SUB, :].rearrange("p (j f) -> p j f", j=NJ),
                                            t.bm1[0:SUB, :].unsqueeze(1).to_broadcast([SUB, NJ, P]),
                                            ALU.add).then_inc(y_ready, 1)
            node_sweep(dve, step, m.NB, 4)


def third_nodes(nc, m, d, t, sb, pb, sem):
    base = sb("base", [SUB, 2, NJ, P], FP32)
    total = sb("total", [P, 2, NJ, SUB], FP32)
    p_out = [pb("p_out0", [P, 512], FP32), pb("p_out1", [P, 512], FP32)]
    k = norm_buffers(sb, sem)
    base_in, stored = [sem("base_in0"), sem("base_in1")], [sem("stored0"), sem("stored1")]
    total_ready, out_summed = sem("total_ready"), sem("out_summed")

    with nc.Block() as block:
        @block.sync
        def _(sp):
            def step(n, slot, turn):
                now = block_before(n, slot, turn, 0, m.NB)
                if now:
                    wait_for(sp, k.u_ready, n - 1)
                    copy_rows(sp, base[:, slot].rearrange("p j f -> p (j f)"), node_rows(d["base"], n), base_in[slot])
                late = block_before(n, slot, turn, 3, m.NB)
                if late:
                    b, s, _ = late
                    sp.wait_ge(k.normed_ready, b + 1)
                    copy_rows(sp, node_rows(d["out"], b), k.normed[:, s].rearrange("p j f -> p (j f)"), stored[s])
            node_sweep(sp, step, m.NB, 3)
            for slot in range(2):
                sp.wait_ge(stored[slot], 32 * ((m.NB + 1 - slot) // 2))

        @block.gpsimd
        def _(pool):
            def step(n, slot, turn):
                wait_for(pool, out_summed, n - 1)
                nc.gpsimd.tensor_copy(total[:, slot], t.sums[:, ds(n * BLOCK, BLOCK)].rearrange("f (p j) -> f j p", j=NJ)
                                      ).then_inc(total_ready, 1)
            node_sweep(pool, step, m.NB)

        @block.scalar
        def _(act):
            def step(n, slot, turn):
                norm_std(nc, act, t, k, n, slot)
            node_sweep(act, step, m.NB)

        @block.tensor
        def _(pe):
            def step(n, slot, turn):
                pe.wait_ge(total_ready, n + 1)
                wait_for(pe, k.u_ready, n - 1)
                for j in range(NJ):
                    last = nc.tensor.matmul(p_out[slot][0:SUB, j * P:(j + 1) * P], total[:, slot, j, :], t.Wm2[:],
                                            start=True, stop=True)
                last.then_inc(out_summed, 1)
            node_sweep(pe, step, m.NB)

        @block.vector
        def _(dve):
            def step(n, slot, turn):
                now = block_before(n, slot, turn, 0, m.NB)
                if now:
                    b, s, use = now
                    dve.wait_ge(out_summed, b + 1)
                    dve.wait_ge(base_in[s], use * 32 + 32)
                    wait_for(dve, k.normed_ready, b - 1)
                    nc.vector.tensor_tensor(k.u[:, s].rearrange("p j f -> p (j f)"), p_out[s][0:SUB, :],
                                            base[:, s].rearrange("p j f -> p (j f)"), ALU.add).then_inc(k.u_ready, 1)
                    norm_moments(nc, dve, k, b, s)
                late = block_before(n, slot, turn, 1, m.NB)
                if late:
                    b, s, use = late
                    wait_for(dve, stored[s], use * 32)
                    norm_apply(nc, dve, k, b, s)
            node_sweep(dve, step, m.NB, 1)


def sum_messages(nc, m, d, t, sb, pb, sem):
    A = d["attr"].shape[1]
    idx = sb("idx", [P, UNROLL, TILES], I32)
    rows = sb("rows", [P, UNROLL, TILES, P], FP32)
    hot = sb("hot", [P, UNROLL, TILES, WIN], FP32)
    attr = sb("attr", [P, UNROLL, TILES, A], FP32)
    when = sb("when", [9, UNROLL, GROUP], BF16)
    wide = 3 * P
    attrT = sb("attrT", [A, 2, wide], FP32)
    hid = sb("hid", [P, 2, wide], FP32)
    gate = sb("gate", [P, 2, wide], FP32)
    gated = sb("gated", [P, 2, wide], FP32)
    p_attr, p_hid, p_edge = pb("p_attr", [P, 512], FP32), pb("p_hid", [P, 512], FP32), pb("p_edge", [P, 512], FP32)
    p_time, p_msg = pb("p_time", [P, 512], FP32), pb("p_msg", [P, 512], FP32)
    win = [pb("win0", [P, 512], FP32), pb("win1", [P, 512], FP32)]
    idx_loaded, gathers_started = sem("idx_loaded"), sem("gathers_started")
    rows_arrived = [[sem(f"rows_arrived{q}_{j}") for j in range(TILES)] for q in range(UNROLL)]
    attr_arrived = [sem(f"attr_arrived{q}") for q in range(UNROLL)]
    when_arrived = [sem(f"when_arrived{q}") for q in range(UNROLL)]
    hot_ready, sums_ready, window_added = sem("hot_ready"), sem("sums_ready"), sem("window_added")
    chain, base_ready = sem("chain"), sem("base_ready")
    attr_flipped, attr_copied = sem("attr_flipped"), sem("attr_copied")
    hid_summed, hid_ready = sem("hid_summed"), sem("hid_ready")
    edge_summed, time_summed, gate_ready, gated_ready = sem("edge_summed"), sem("time_summed"), sem("gate_ready"), sem("gated_ready")
    msg_summed, msg_added, msg_ready = sem("msg_summed"), sem("msg_added"), sem("msg_ready")
    sems = [idx_loaded, gathers_started, *[a for slot in rows_arrived for a in slot], *attr_arrived, *when_arrived, hot_ready, sums_ready,
            window_added, chain, base_ready, attr_flipped, attr_copied, hid_summed, hid_ready, edge_summed,
            time_summed, gate_ready, gated_ready, msg_summed, msg_added, msg_ready]
    NC = 2 * m.NG
    attr_d = d["attr"].rearrange("(g p j) a -> g p (j a)", p=P, j=TILES)

    def chunk(i, q, lag):
        found = item(i, q, lag, CHUNKS, NC)
        if found is None:
            return None
        c, body, at = found
        k = Names()
        k.c, k.buf, k.first = c, at % 2, at % 2 == 0
        k.group, k.body, k.slot = body * UNROLL + at // 2, body, at // 2
        k.t0, k.t1 = CHUNK_TILES[at % 2]
        k.nt = k.t1 - k.t0
        k.w = k.nt * P
        return k

    def one_pass():
        with nc.Block() as block:
            @block.gpsimd
            def _(pool):
                gather_groups(nc, pool, m, d["y"], idx, rows, idx_loaded, sums_ready, gathers_started, rows_arrived)

            @block.sync
            def _(sp):
                def step(i, q):
                    g = i * UNROLL + q
                    wait_for(sp, attr_flipped, g * 2 - 2 * UNROLL + 2)
                    sp.dma_start(attr[:, q].rearrange("p j a -> p (j a)"),
                                 attr_d[ds(g, 1), :, :].rearrange("o p c -> (o p) c")).then_inc(attr_arrived[q], 16)
                    wait_for(sp, time_summed, g * 2 - 2 * UNROLL + 2)
                    for c in range(3):
                        sp.dma_start(when[3 * c:3 * c + 3, q, :],
                                     d["weight_parts"][c:c + 1, ds(g * GROUP, GROUP)].to_broadcast([3, GROUP])
                                     ).then_inc(when_arrived[q], 16)
                edge_sweep(sp, step, m.NG, UNROLL, 0)

            @block.tensor
            def _(pe):
                def step(i, q):
                    k = chunk(i, q, 0)
                    if k:
                        pe.wait_ge(attr_arrived[k.slot], k.body * 16 + 16)
                        wait_for(pe, attr_copied, k.c)
                    k = chunk(i, q, 1)
                    if k:
                        pe.wait_ge(attr_copied, k.c + 1)
                        wait_for(pe, hid_ready, k.c)
                        nc.tensor.matmul(p_hid[:, 0:k.w], t.We1[:], attrT[:, k.buf, 0:k.w], start=True, stop=True
                                         ).then_inc(hid_summed, 1)
                    k = chunk(i, q, 0)
                    if k:
                        for j in range(k.t0, k.t1):
                            last = nc.tensor.transpose(p_attr[0:A, (j - k.t0) * P:(j - k.t0 + 1) * P], attr[:, k.slot, j, :],
                                                       t.identity[:])
                        last.then_inc(attr_flipped, 1)
                    k = chunk(i, q, 2)
                    if k:
                        pe.wait_ge(when_arrived[k.slot], k.body * 48 + 48)
                        wait_for(pe, gate_ready, k.c)
                        nc.tensor.matmul(p_time[:, 0:k.w].rearrange("f (j p) -> f j p", p=P), t.Wt9[:],
                                         when[:, k.slot, :].rearrange("r (p j) -> r j p", j=TILES)[:, k.t0:k.t1, :],
                                         start=True, stop=True).then_inc(time_summed, 1)
                        pe.wait_ge(hid_ready, k.c + 1)
                        wait_for(pe, gated_ready, k.c)
                        nc.tensor.matmul(p_edge[:, 0:k.w], t.We2[:], hid[:, k.buf, 0:k.w], start=True, stop=True
                                         ).then_inc(edge_summed, 1)
                    k = chunk(i, q, 3)
                    if k:
                        pe.wait_ge(gated_ready, k.c + 1)
                        wait_for(pe, msg_added, k.c)
                        for j in range(k.nt):
                            last = nc.tensor.matmul(p_msg[:, j * P:(j + 1) * P], gated[:, k.buf, j * P:(j + 1) * P], t.Wm_e[:],
                                                    start=True, stop=True)
                        last.then_inc(msg_summed, 1)
                    k = chunk(i, q, 6)
                    if k and k.first:
                        pe.wait_ge(msg_ready, k.c + 2)
                        pe.wait_ge(hot_ready, k.group + 1)
                        wait_for(pe, window_added, k.group if k.slot == 0 else k.group - 1)
                        for j in range(TILES):
                            last = nc.tensor.matmul(win[k.slot % 2][:, 0:WIN], rows[:, k.slot, j, :], hot[:, k.slot, j, :],
                                                    start=j == 0, stop=j == TILES - 1)
                        last.then_inc(sums_ready, 1)
                edge_sweep(pe, step, NC, CHUNKS, 7)

            @block.scalar
            def _(act):
                def step(i, q):
                    k = chunk(i, q, 0)
                    if k and k.first:
                        wait_for(act, msg_added, k.c - 2 * UNROLL + 2)
                        nc.scalar.copy(idx[:, k.slot, :], t.src_idx[:, ds(k.group, 1), :].rearrange("p o j -> p (o j)")
                                       ).then_inc(idx_loaded, 1)
                    if k:
                        act.wait_ge(attr_flipped, k.c + 1)
                        wait_for(act, hid_summed, k.c - 1)
                        nc.scalar.copy(attrT[:, k.buf, 0:k.w], p_attr[0:A, 0:k.w]).then_inc(attr_copied, 1)
                    k = chunk(i, q, 1)
                    if k:
                        act.wait_ge(hid_summed, k.c + 1)
                        wait_for(act, edge_summed, k.c - 1)
                        nc.scalar.activation(hid[:, k.buf, 0:k.w], p_hid[:, 0:k.w], ACT.Relu, bias=t.be1[:, 0:1]
                                             ).then_inc(hid_ready, 1)
                    k = chunk(i, q, 2)
                    if k:
                        act.wait_ge(time_summed, k.c + 1)
                        wait_for(act, gated_ready, k.c - 1)
                        nc.scalar.activation(gate[:, k.buf, 0:k.w], p_time[:, 0:k.w], ACT.Sigmoid, bias=t.bt[:, 0:1]
                                             ).then_inc(gate_ready, 1)
                    k = chunk(i, q, 4)
                    if k:
                        act.wait_ge(msg_added, k.c + 1)
                        nc.scalar.activation(rows[:, k.slot, k.t0:k.t1, :], rows[:, k.slot, k.t0:k.t1, :], ACT.Relu
                                             ).then_inc(msg_ready, 1)
                edge_sweep(act, step, NC, CHUNKS, 4)

            @block.vector
            def _(dve):
                set_windows(nc, dve, m, t, chain, base_ready)

                def step(i, q):
                    k = chunk(i, q, 2)
                    if k:
                        dve.wait_ge(gate_ready, k.c + 1)
                        dve.wait_ge(edge_summed, k.c + 1)
                        wait_for(dve, msg_summed, k.c - 1)
                        nc.vector.scalar_tensor_tensor(gated[:, k.buf, 0:k.w], p_edge[:, 0:k.w], t.be2[:, 0:1],
                                                       gate[:, k.buf, 0:k.w], ALU.add, ALU.mult).then_inc(gated_ready, 1)
                    k = chunk(i, q, 3)
                    if k:
                        for j in range(k.t0, k.t1):
                            dve.wait_ge(rows_arrived[k.slot][j], k.body * 16 + 16)
                        dve.wait_ge(msg_summed, k.c + 1)
                        at = rows[:, k.slot, k.t0:k.t1, :].rearrange("p j f -> p (j f)")
                        nc.vector.tensor_tensor(at, p_msg[:, 0:k.w], at, ALU.add).then_inc(msg_added, 1)
                    k = chunk(i, q, 4)
                    if k and k.first:
                        wait_for(dve, sums_ready, k.group - UNROLL + 1)
                        one_hot(nc, t, hot, k.group, k.slot).then_inc(hot_ready, 1)
                    k = chunk(i, q, 7)
                    if k and k.first:
                        base = dve.value_load(t.base_int[0:1, ds(k.group, 1)], min_val=0, max_val=m.N)
                        wait_for(dve, window_added, k.group)
                        dve.wait_ge(sums_ready, k.group + 1)
                        w = ds(base, WIN)
                        nc.vector.tensor_tensor(t.sums[:, w], t.sums[:, w], win[k.slot % 2][:, 0:WIN],
                                                ALU.add).then_inc(window_added, 1)
                edge_sweep(dve, step, NC, CHUNKS, 8)
        clear_counts(nc, sems, gathered=True)

    all_passes(nc, m, t, one_pass)


def gnn(nc, d):
    m = Names()
    m.N, F = d["x"].shape
    m.E = d["src"].shape[0]
    m.H = d["Ws1"].shape[1]
    m.NG = m.E // GROUP
    m.NB = m.N // BLOCK
    assert F == P and m.NG * GROUP == m.E and m.NG % UNROLL == 0 and m.NB * BLOCK == m.N and m.E % (SUB * GROUP) == 0
    m.WINDOWS = -(-m.N // WIN)
    d["low"], d["span"] = (nc.dram_tensor(n, [m.NG], FP32).ap() for n in ("group_low", "group_span"))
    d["degree"], d["inv_degree"] = (nc.dram_tensor(n, [m.N], FP32).ap() for n in ("degree_d", "inv_degree_d"))
    d["weight_parts"] = nc.dram_tensor("weight_parts", [3, m.E], BF16).ap()
    d["wt_parts"] = nc.dram_tensor("wt_parts_d", [3, P], BF16).ap()
    d["z"], d["own"], d["base"], d["y"] = (nc.dram_tensor(n, [m.N, P], FP32).ap() for n in ("z_d", "own_d", "base_d", "y_d"))

    with ExitStack() as whole:
        def run(tag, build, *args):
            with ExitStack() as part:
                sems = []

                def sem(name):
                    sems.append(part.enter_context(nc.semaphore(tag + name)))
                    return sems[-1]

                build(*args, lambda n, s, dt: part.enter_context(nc.sbuf_tensor(tag + n, s, dt)),
                      lambda n, s, dt: part.enter_context(nc.psum_tensor(tag + n, s, dt)), sem)
                clear_counts(nc, sems)

        def sb(name, shape, dt):
            return whole.enter_context(nc.sbuf_tensor(name, shape, dt))

        t = Names()
        t.rel = sb("rel", [P, m.NG, TILES], FP32)
        t.src_idx = sb("src_idx", [P, m.NG, TILES], I32)
        t.fast_base, t.base_now, t.base_next = (sb(n, [P, m.NG], FP32) for n in ("fast_base", "base_now", "base_next"))
        t.base_int = sb("base_int", [1, m.NG], I32)
        t.passes = sb("passes", [1, 1], I32)
        t.slow_base, t.window_step = sb("slow_base", [P, 1], FP32), sb("window_step", [P, 1], FP32)
        t.identity = sb("identity", [P, P], FP32)
        t.ones, t.ones_row, t.eps = sb("ones", [P, 1], FP32), sb("ones_row", [1, P], FP32), sb("eps", [P, 1], FP32)
        t.We1 = sb("We1", list(d["We1"].shape), FP32)
        t.We2, t.Wm_x, t.Wm_e, t.Wm2 = (sb(n, [P, P], FP32) for n in ("We2", "Wm_x", "Wm_e", "Wm2"))
        t.Ws1, t.Wn1 = sb("Ws1", [P, m.H], FP32), sb("Wn1", [P, m.H], FP32)
        t.Wn2a, t.Ws2a = sb("Wn2a", [P, P], FP32), sb("Ws2a", [P, P], FP32)
        t.Wn2b, t.Ws2b = sb("Wn2b", [m.H - P, P], FP32), sb("Ws2b", [m.H - P, P], FP32)
        t.b1a, t.b1b = sb("b1a", [P, 1], FP32), sb("b1b", [m.H - P, 1], FP32)
        t.be1, t.be2, t.bt = (sb(n, [P, 1], FP32) for n in ("be1", "be2", "bt"))
        t.b2, t.bm1, t.bm2 = (sb(n, [P, P], FP32) for n in ("b2", "bm1", "bm2"))
        t.Wt9 = sb("Wt9", [9, P], BF16)
        t.degree_n, t.inv_n, t.has_n = (sb(n, [SUB, m.NB, NJ], FP32) for n in ("degree_n", "inv_n", "has_n"))
        t.iota_ps = whole.enter_context(nc.psum_tensor("iota_ps", [P, 512], FP32))

        t.zeros = sb("zeros", [P, BLOCK], FP32)
        t.sums = sb("sums", [P, m.N + WIN], FP32)
        run("load_", load_and_index, nc, m, d, t)
        with nc.sbuf_tensor("degree", [1, m.N + WIN], FP32) as degree:
            with nc.Block() as block:
                @block.vector
                def _(dve):
                    nc.vector.memset(degree[:], 0.0)
            run("sum_x_", sum_neighbours, nc, m, t, d["x"], degree)
            run("degree_", invert_degrees, nc, m, d, t, degree)
        run("first_", first_nodes, nc, m, d, t)
        run("sum_z_", sum_neighbours, nc, m, t, d["z"], None)
        run("second_", second_nodes, nc, m, d, t)
        run("messages_", sum_messages, nc, m, d, t)
        run("third_", third_nodes, nc, m, d, t)


INPUTS = {
    "x": "x", "src": "src", "dst": "dst", "edge_attr_64": "attr", "edge_weight": "edge_weight",
    "L0_gnn_W_self1": "Ws1", "L0_gnn_W_neigh1": "Wn1", "L0_gnn_b1": "b1",
    "L0_gnn_W_self2": "Ws2", "L0_gnn_W_neigh2": "Wn2", "L0_gnn_b2": "b2",
    "L1_gnn_We1": "We1", "L1_gnn_be1": "be1", "L1_gnn_We2": "We2", "L1_gnn_be2": "be2",
    "L1_gnn_Wt": "Wt", "L1_gnn_bt": "bt", "L1_gnn_Wn1": "Wm1", "L1_gnn_bn1": "bm1",
    "L1_gnn_Wn2": "Wm2", "L1_gnn_bn2": "bm2",
}


def kernel(**inputs):
    import numpy as np
    import concourse.bacc as bacc
    from concourse.bass_utils import run_bass_kernel_spmd

    nc = bacc.Bacc("TRN2", target_bir_lowering=False, num_devices=1)
    arrays, d = {}, {}
    for name, short in INPUTS.items():
        a = np.ascontiguousarray(inputs[name])
        arrays[f"in_{name}"] = a
        ap = nc.dram_tensor(f"in_{name}", a.shape, mybir.dt.from_np(a.dtype), kind="ExternalInput").ap()
        d[short] = ap
    d["out"] = nc.dram_tensor("out", list(inputs["x"].shape), FP32, kind="ExternalOutput").ap()
    gnn(nc, d)
    got = run_bass_kernel_spmd(nc, [arrays], core_ids=[0])
    return got.results[0]["out"]
```

```python
from contextlib import ExitStack

import concourse.bass as bass
from concourse import mybir

FP32 = mybir.dt.float32
BF16 = mybir.dt.bfloat16
I32 = mybir.dt.int32
ALU = mybir.AluOpType
ACT = mybir.ActivationFunctionType
AX = mybir.AxisListType
ds = bass.ds

P = 128
TILES = 5
GROUP = TILES * P
UNROLL = 5
WIN = 64
BLOCK = 500
SUB = 125
NJ = BLOCK // SUB
CHUNKS = 2 * UNROLL
CHUNK_TILES = ((0, 3), (3, 5))
PARTS = 2
PIECE = PARTS * P
EPS = 1e-5


class Names:
    pass


def wait_for(eng, sem, count):
    if isinstance(count, int) and count < 1:
        return
    eng.wait_ge(sem, count)


def copy_rows(eng, out, in_, sem):
    for a, b in ((0, 112), (112, SUB)):
        eng.dma_start(out[a:b], in_[a:b]).then_inc(sem, 16)


def edge_sweep(eng, step, total, unroll, lag, peel=2):
    for i in range(peel):
        for q in range(unroll):
            step(i, q)
    with eng.Fori(peel, total // unroll) as i:
        for q in range(unroll):
            step(i, q)
    for q in range(lag):
        step(total // unroll + q // unroll, q % unroll)


def item(i, q, lag, unroll, total):
    if q < lag:
        i, q = i - 1, q + unroll
    n = i * unroll + q - lag
    if isinstance(n, int) and not 0 <= n < total:
        return None
    return n, i, q - lag


def node_sweep(eng, step, total, lag=0):
    peel = 9
    for n in range(peel):
        step(n, n % 2, n // 2)
    with eng.Fori(0, (total - peel) // 2) as i:
        for q in range(2):
            step(i * 2 + (peel + q), (peel + q) % 2, i + (peel + q) // 2)
    for n in range(total, total + lag):
        step(n, n % 2, n // 2)


def block_before(n, slot, turn, lag, total):
    m = n - lag
    if isinstance(m, int):
        return (m, m % 2, m // 2) if 0 <= m < total else None
    if lag % 2 == 0:
        return m, slot, turn - lag // 2
    return m, 1 - slot, turn - (lag + 1) // 2 + slot


def load_and_index(nc, m, d, t, sb, pb, sem):
    rows = m.E // SUB
    dst_i, src_i = sb("dst_i", [SUB, rows], I32), sb("src_i", [SUB, rows], I32)
    dst_f, src_f = dst_i[:].bitcast(FP32), src_i[:].bitcast(FP32)
    rest = sb("rest", [SUB, rows], FP32)
    parts = sb("parts", [SUB, 3, rows], BF16)
    wt_row = sb("wt_row", [1, P], FP32)
    wt_parts = sb("wt_parts", [1, 3, P], BF16)
    groups_row = rows // GROUP
    low = sb("low", [SUB, groups_row], FP32)
    span = sb("span", [SUB, groups_row], FP32)
    span_all = sb("span_all", [P, m.NG], FP32)
    widest = sb("widest", [P, 1], FP32)
    is_slow, is_fast = sb("is_slow", [P, 1], FP32), sb("is_fast", [P, 1], FP32)
    passes_f, again_f, most = (sb(n, [1, 1], FP32) for n in ("passes_f", "again_f", "most"))
    falls = sb("falls", [1, m.NG - 1], FP32)
    start_f, steps, every_f = (sb(n, [1, m.PIECES], FP32) for n in ("start_f", "steps", "every_f"))
    every_i = sb("every_i", [1, m.PIECES], I32)
    iota_i, iota_f = sb("iota_i", [1, WIN], I32), sb("iota_f", [1, WIN], FP32)
    FLIPS = 4
    flip = [pb(f"flip{n}", [P, 512], FP32) for n in range(FLIPS)]
    dst_in, src_in, weight_in, params_in = sem("dst_in"), sem("src_in"), sem("weight_in"), sem("params_in")
    identity_ready, iota_ready, ones_ready = sem("identity_ready"), sem("iota_ready"), sem("ones_ready")
    dst_float, src_float, iota_float = sem("dst_float"), sem("src_float"), sem("iota_float")
    low_ready, part_cut, part_taken, wt_ready = sem("low_ready"), sem("part_cut"), sem("part_taken"), sem("wt_ready")
    low_stored, parts_stored, wt_stored = sem("low_stored"), sem("parts_stored"), sem("wt_stored")
    low_back, wt_back = sem("low_back"), sem("wt_back")
    flipped, even_copied, odd_copied = sem("flipped"), sem("even_copied"), sem("odd_copied")
    chain, pool_chain, iota_spread = sem("chain"), sem("pool_chain"), sem("iota_spread")

    flips = [(src, out, k, j) for src, out in ((src_f, t.src_idx), (dst_f, t.rel))
             for k in range(groups_row) for j in range(TILES)]

    def take_flip(copy, n):
        _, out, k, j = flips[n]
        return copy(out[:].rearrange("p (q k) j -> p q k j", k=groups_row)[:, :, k, j], flip[n % FLIPS][:, 0:SUB])

    with nc.Block() as block:
        @block.sync
        def _(sp):
            copy_rows(sp, src_i, d["src"].rearrange("(q r) -> q r", q=SUB), src_in)
            copy_rows(sp, dst_i, d["dst"].rearrange("(q r) -> q r", q=SUB), dst_in)
            copy_rows(sp, rest, d["edge_weight"].rearrange("(q r) -> q r", q=SUB), weight_in)
            sp.dma_start(wt_row[:], d["Wt"]).then_inc(weight_in, 16)
            sp.wait_ge(low_ready, 1)
            sp.dma_start(d["low"].rearrange("(q k) -> q k", q=SUB), low[:]).then_inc(low_stored, 16)
            sp.dma_start(d["span"].rearrange("(q k) -> q k", q=SUB), span[:]).then_inc(low_stored, 16)
            sp.wait_ge(low_stored, 32)
            sp.dma_start(t.fast_base[:], d["low"].partition_broadcast(P)).then_inc(low_back, 16)
            sp.dma_start(span_all[:], d["span"].partition_broadcast(P)).then_inc(low_back, 16)
            sp.wait_ge(wt_ready, 1)
            sp.dma_start(d["wt_parts"].rearrange("(o c) f -> o c f", o=1), wt_parts[:]).then_inc(wt_stored, 16)
            sp.wait_ge(wt_stored, 16)
            for c in range(3):
                sp.dma_start(t.Wt9[3 * c:3 * c + 3, :], d["wt_parts"]).then_inc(wt_back, 16)
            for c in range(3):
                sp.wait_ge(part_cut, c + 1)
                copy_rows(sp, d["weight_parts"][c, :].rearrange("(q r) -> q r", q=SUB), parts[:, c, :], parts_stored)
            sp.wait_ge(wt_back, 48)
            sp.wait_ge(low_back, 32)
            sp.wait_ge(parts_stored, 96)

        @block.scalar
        def _(act):
            act.wait_ge(src_in, 32)
            nc.scalar.copy(src_f, src_i[:]).then_inc(src_float, 1)
            loads = [
                (t.We1[:], d["We1"]), (t.We2[:], d["We2"]), (t.Wm_x[:], d["Wm1"][0:P, :]), (t.Wm_e[:], d["Wm1"][P:2 * P, :]),
                (t.Wm2[:], d["Wm2"]), (t.Ws1[:], d["Ws1"]), (t.Wn1[:], d["Wn1"]),
                (t.Wn2a[:], d["Wn2"][0:P, :]), (t.Wn2b[:], d["Wn2"][P:m.H, :]),
                (t.Ws2a[:], d["Ws2"][0:P, :]), (t.Ws2b[:], d["Ws2"][P:m.H, :]),
                (t.b1a[:], d["b1"][0:P].rearrange("(f o) -> f o", o=1)), (t.b1b[:], d["b1"][P:m.H].rearrange("(f o) -> f o", o=1)),
                (t.be1[:], d["be1"].rearrange("(f o) -> f o", o=1)), (t.be2[:], d["be2"].rearrange("(f o) -> f o", o=1)),
                (t.bt[:], d["bt"].rearrange("(f o) -> f o", o=1)),
                (t.b2[:], d["b2"].partition_broadcast(P)), (t.bm1[:], d["bm1"].partition_broadcast(P)),
                (t.bm2[:], d["bm2"].partition_broadcast(P)),
            ]
            for out, in_ in loads:
                act.dma_start(out, in_).then_inc(params_in, 16)
            for n in range(0, len(flips), 2):
                act.wait_ge(flipped, n + 1)
                take_flip(nc.scalar.copy, n).then_inc(even_copied, 1)
            act.wait_ge(weight_in, 48)
            for c in range(3):
                if c > 0:
                    act.wait_ge(part_taken, c)
                nc.scalar.copy(parts[:, c, :], rest[:]).then_inc(part_cut, 1)
            act.wait_ge(params_in, 16 * len(loads))

        @block.gpsimd
        def _(pool):
            nc.gpsimd.memset(t.identity[:], 0.0).then_inc(pool_chain, 1)
            pool.wait_ge(pool_chain, 1)
            nc.gpsimd.affine_select(out=t.identity[:], in_=t.identity[:], compare_op=ALU.not_equal, fill=1.0,
                                    base=0, pattern=[[-1, P]], channel_multiplier=1).then_inc(identity_ready, 1)
            nc.gpsimd.iota(iota_i[:], pattern=[[1, WIN]], base=0, channel_multiplier=0).then_inc(iota_ready, 1)
            nc.gpsimd.iota(every_i[:], pattern=[[PIECE, m.PIECES]], base=0, channel_multiplier=0).then_inc(iota_ready, 1)
            nc.gpsimd.memset(t.ones[:], 1.0).then_inc(ones_ready, 1)
            nc.gpsimd.memset(t.ones_row[:], 1.0).then_inc(ones_ready, 1)
            nc.gpsimd.memset(t.eps[:], EPS).then_inc(ones_ready, 1)
            nc.gpsimd.memset(t.zeros[:], 0.0).then_inc(ones_ready, 1)
            nc.gpsimd.memset(t.sums[:], 0.0).then_inc(ones_ready, 1)

        @block.vector
        def _(dve):
            done = [0]

            def then(ins):
                done[0] += 1
                ins.then_inc(chain, 1)
                dve.wait_ge(chain, done[0])

            dve.wait_ge(iota_ready, 2)
            then(nc.vector.tensor_copy(every_f[:], every_i[:]))
            then(nc.vector.tensor_scalar(every_f[:], every_f[:], float(m.N - PIECE), None, ALU.min))
            then(nc.vector.tensor_copy(t.every_start[:], every_f[:]))
            nc.vector.tensor_copy(iota_f[:], iota_i[:]).then_inc(iota_float, 1)
            for n in range(1, len(flips) // 2, 2):
                dve.wait_ge(flipped, n + 1)
                take_flip(nc.vector.tensor_copy, n).then_inc(odd_copied, 1)
            dve.wait_ge(dst_in, 32)
            nc.vector.tensor_copy(dst_f, dst_i[:]).then_inc(dst_float, 1)
            dve.wait_ge(dst_float, 1)
            by_group = dst_f.rearrange("q (k e) -> q k e", e=GROUP)
            then(nc.vector.tensor_reduce(low[:], by_group, axis=AX.X, op=ALU.min))
            then(nc.vector.tensor_reduce(span[:], by_group, axis=AX.X, op=ALU.max))
            nc.vector.tensor_tensor(span[:], span[:], low[:], ALU.subtract).then_inc(low_ready, 1)
            for n in range(len(flips) // 2 + (len(flips) // 2 + 1) % 2, len(flips), 2):
                dve.wait_ge(flipped, n + 1)
                take_flip(nc.vector.tensor_copy, n).then_inc(odd_copied, 1)
            dve.wait_ge(weight_in, 48)
            then(nc.vector.tensor_copy(wt_parts[:, 0, :], wt_row[:]))
            then(nc.vector.tensor_tensor(wt_row[:], wt_row[:], wt_parts[:, 0, :], ALU.subtract))
            then(nc.vector.tensor_copy(wt_parts[:, 1, :], wt_row[:]))
            then(nc.vector.tensor_tensor(wt_row[:], wt_row[:], wt_parts[:, 1, :], ALU.subtract))
            nc.vector.tensor_copy(wt_parts[:, 2, :], wt_row[:]).then_inc(wt_ready, 1)
            for c in range(2):
                dve.wait_ge(part_cut, c + 1)
                nc.vector.tensor_tensor(rest[:], rest[:], parts[:, c, :], ALU.subtract).then_inc(part_taken, 1)
            dve.wait_ge(low_back, 32)
            then(nc.vector.tensor_reduce(widest[:], span_all[:], axis=AX.X, op=ALU.max))
            then(nc.vector.tensor_scalar(is_slow[:], widest[:], float(WIN), None, ALU.is_ge))
            then(nc.vector.tensor_scalar(is_fast[:], widest[:], float(WIN), None, ALU.is_lt))
            then(nc.vector.tensor_scalar(t.window_step[:], is_slow[:], float(WIN), None, ALU.mult))
            then(nc.vector.memset(start_f[:, m.PIECES - 1:m.PIECES], float(m.N - PIECE)))
            then(nc.vector.tensor_scalar(start_f[:, 0:m.PIECES - 1],
                                         t.fast_base[0:1, :].rearrange("o (i q) -> o i q", q=UNROLL)[:, 1:, 0],
                                         float(-PIECE), 0.0, ALU.add, ALU.max))
            then(nc.vector.tensor_copy(t.piece_start[:], start_f[:]))
            then(nc.vector.tensor_scalar(steps[:, 0:1], start_f[:, 0:1], 0.0, None, ALU.is_gt))
            then(nc.vector.tensor_tensor(steps[:, 1:], start_f[:, 1:], start_f[:, 0:m.PIECES - 1], ALU.subtract))
            then(nc.vector.tensor_scalar(steps[:, 1:], steps[:, 1:], float(PIECE), None, ALU.is_gt))
            then(nc.vector.tensor_reduce(again_f[:], steps[:], axis=AX.X, op=ALU.max))
            then(nc.vector.tensor_tensor(falls[:], t.fast_base[0:1, 0:m.NG - 1], t.fast_base[0:1, 1:], ALU.is_gt))
            then(nc.vector.tensor_reduce(most[:], falls[:], axis=AX.X, op=ALU.max))
            then(nc.vector.tensor_tensor(again_f[:], again_f[:], most[:], ALU.max))
            then(nc.vector.tensor_tensor(again_f[:], again_f[:], is_slow[0:1, :], ALU.max))
            then(nc.vector.tensor_copy(t.again[:], again_f[:]))
            then(nc.vector.tensor_scalar(t.fast_base[:], t.fast_base[:], is_fast[:, 0:1], None, ALU.mult))
            then(nc.vector.tensor_scalar(passes_f[:], is_slow[0:1, :], float(m.WINDOWS - 1), 1.0, ALU.mult, ALU.add))
            then(nc.vector.tensor_copy(t.passes[:], passes_f[:]))
            then(nc.vector.memset(t.base_now[:], 0.0))
            then(nc.vector.memset(t.slow_base[:], 0.0))

        @block.tensor
        def _(pe):
            pe.wait_ge(ones_ready, 2)
            pe.wait_ge(iota_float, 1)
            nc.tensor.matmul(t.iota_ps[:, 0:WIN], t.ones_row[:], iota_f[:], start=True, stop=True).then_inc(iota_spread, 1)
            pe.wait_ge(identity_ready, 1)
            pe.wait_ge(src_float, 1)
            for n, (source, _, k, j) in enumerate(flips):
                if n == len(flips) // 2:
                    pe.wait_ge(dst_float, 1)
                if n >= FLIPS:
                    pe.wait_ge(odd_copied if n % 2 else even_copied, (n - FLIPS) // 2 + 1)
                nc.tensor.transpose(flip[n % FLIPS][:, 0:SUB],
                                    source.rearrange("q (k p j) -> q k j p", p=P, j=TILES)[:, k, j, :],
                                    t.identity[0:SUB, 0:SUB]).then_inc(flipped, 1)
            pe.wait_ge(iota_spread, 1)


def set_windows(nc, dve, m, t, chain, base_ready):
    done = [0]

    def then(ins):
        done[0] += 1
        ins.then_inc(chain, 1)
        dve.wait_ge(chain, done[0])

    then(nc.vector.tensor_scalar(t.base_next[:], t.fast_base[:], t.slow_base[:, 0:1], None, ALU.add))
    then(nc.vector.tensor_tensor(t.base_now[:], t.base_now[:], t.base_next[:], ALU.subtract))
    then(nc.vector.tensor_tensor(t.rel[:], t.rel[:], t.base_now[:].unsqueeze(2).to_broadcast([P, m.NG, TILES]), ALU.add))
    then(nc.vector.tensor_copy(t.base_now[:], t.base_next[:]))
    then(nc.vector.tensor_tensor(t.slow_base[:], t.slow_base[:], t.window_step[:], ALU.add))
    nc.vector.tensor_copy(t.base_int[:], t.base_next[0:1, :]).then_inc(base_ready, 1)
    dve.wait_ge(base_ready, 1)


def one_hot(nc, t, hot, g, slot):
    return nc.vector.tensor_tensor(
        hot[:, slot],
        t.iota_ps[:, 0:WIN].unsqueeze(1).to_broadcast([P, TILES, WIN]),
        t.rel[:, ds(g, 1), :].rearrange("p o j -> p (o j)").unsqueeze(2).to_broadcast([P, TILES, WIN]), ALU.is_equal)


def gather_groups(nc, pool, m, table, idx, rows, idx_loaded, sums_ready, gathers_started, rows_arrived):
    def step(i, q):
        g = i * UNROLL + q
        wait_for(pool, sums_ready, g - UNROLL + 1)
        pool.wait_ge(idx_loaded, g + 1)
        pool.sem_inc(gathers_started, 1)
        for j in range(TILES):
            nc.gpsimd.indirect_dma_start(
                out=rows[:, q, j, :], out_offset=None, in_=table,
                in_offset=bass.IndirectOffsetOnAxis(ap=idx[:, q, j:j + 1], axis=0)).then_inc(rows_arrived[q][j], 16)
    edge_sweep(pool, step, m.NG, UNROLL, 0)
    for slot in rows_arrived:
        for tile_arrived in slot:
            pool.wait_ge(tile_arrived, m.NG // UNROLL * 16)


def clear_counts(nc, sems, gathered=False):
    if gathered:
        nc.gpsimd.dma_reset()
    for s in sems:
        nc.gpsimd.sem_clear(s)
    nc.all_engine_barrier()


def piece_steps(fn, eng, m, i, q):
    for late in (1, 0):
        k = i - 1 - late
        if not isinstance(k, int) or 0 <= k < m.PIECES:
            fn(eng, k, q + late * UNROLL)


def pieces_alone(nc, m, t, side):
    def every_piece(eng, fn):
        for q in range(2 * UNROLL):
            fn(eng, 0, q)
        with eng.Fori(1, m.PIECES) as k:
            for q in range(2 * UNROLL):
                fn(eng, k, q)

    with nc.Block() as block:
        @block.sync
        def _(sp):
            def move(sp, k, q):
                if q == 0:
                    side.load(sp, k, t.every_start)
                    side.store(sp, k, t.every_start)
            every_piece(sp, move)
            sp.wait_ge(side.stored, side.count * m.PIECES)

        @block.tensor
        def _(pe):
            every_piece(pe, side.tensor)

        @block.scalar
        def _(act):
            every_piece(act, side.scalar)

        @block.vector
        def _(dve):
            every_piece(dve, lambda dve, k, q: side.vector(dve, k, q, t.every_start))

        @block.gpsimd
        def _(pool):
            pool.wait_ge(side.stored, side.count * m.PIECES)
    clear_counts(nc, side.sems)


def piece_start(eng, m, starts, k):
    return eng.value_load(starts[0:1, ds(k, 1)], min_val=0, max_val=m.N - PIECE)


def piece_rows(ap, first):
    return ap[ds(first, PIECE), :].rearrange("(j p) f -> p j f", p=P)


def take_mean(nc, dve, m, t, k, starts, inv, mean, chain, mean_used):
    nodes = ds(piece_start(dve, m, starts, k), PIECE)
    nc.vector.tensor_scalar(inv[:], t.degree[:, nodes], 1.0, None, ALU.max).then_inc(chain, 1)
    dve.wait_ge(chain, k * 2 + 1)
    nc.vector.reciprocal(inv[:], inv[:]).then_inc(chain, 1)
    dve.wait_ge(chain, k * 2 + 2)
    wait_for(dve, mean_used, k)
    return nc.vector.tensor_tensor(mean[:], t.sums[:, nodes], inv[:], ALU.mult)


def first_nodes(nc, m, d, t, sb, pb, sem):
    HB = m.H - P
    x = sb("piece_x", [P, PARTS, P], FP32)
    xT = sb("piece_xT", [P, PIECE], FP32)
    inv, mean = sb("piece_inv", [P, PIECE], FP32), sb("piece_mean", [P, PIECE], FP32)
    hA, hB = sb("piece_hA", [P, PIECE], FP32), sb("piece_hB", [HB, PIECE], FP32)
    z, own = sb("piece_z", [P, PARTS, P], FP32), sb("piece_own", [P, PARTS, P], FP32)
    p_x, p_h, p_out = (pb(n, [P, 512], FP32) for n in ("piece_p_x", "piece_p_h", "piece_p_out"))
    p_hA, p_hB = p_h[:, 0:PIECE], p_h[0:HB, PIECE:2 * PIECE]
    x_in, flipped, copied, chain = sem("x_in"), sem("x_flipped"), sem("x_copied"), sem("inv_chain")
    mean_ready, h_summed, h_ready = sem("mean_ready"), sem("h_summed"), sem("h_ready")
    out_summed, out_ready, storing, stored = sem("out_summed"), sem("out_ready"), sem("storing"), sem("stored")

    def load(sp, k, starts):
        wait_for(sp, flipped, k)
        sp.dma_start(x[:], piece_rows(d["x"], piece_start(sp, m, starts, k))).then_inc(x_in, 16)

    def store(sp, k, starts):
        sp.wait_ge(out_ready, k + 1)
        sp.sem_inc(storing, 1)
        first = piece_start(sp, m, starts, k)
        sp.dma_start(piece_rows(d["z"], first), z[:]).then_inc(stored, 16)
        sp.dma_start(piece_rows(d["own"], first), own[:]).then_inc(stored, 16)

    def tensor(pe, k, q):
        if q == 1:
            pe.wait_ge(x_in, k * 16 + 16)
            wait_for(pe, copied, k)
            for j in range(PARTS):
                last = nc.tensor.transpose(p_x[:, j * P:(j + 1) * P], x[:, j, :], t.identity[:])
            last.then_inc(flipped, 1)
        if q == 3:
            pe.wait_ge(copied, k + 1)
            pe.wait_ge(mean_ready, k + 1)
            wait_for(pe, h_ready, k)
            nc.tensor.matmul(p_hA, t.Ws1[:, 0:P], xT[:], start=True, stop=False)
            nc.tensor.matmul(p_hA, t.Wn1[:, 0:P], mean[:], start=False, stop=True)
            nc.tensor.matmul(p_hB, t.Ws1[:, P:m.H], xT[:], start=True, stop=False)
            nc.tensor.matmul(p_hB, t.Wn1[:, P:m.H], mean[:], start=False, stop=True).then_inc(h_summed, 1)
        if q == 6:
            pe.wait_ge(h_ready, k + 1)
            wait_for(pe, out_ready, k)
            for j in range(PARTS):
                part = slice(j * P, (j + 1) * P)
                p_z, p_own = p_out[:, part], p_out[:, PIECE + j * P:PIECE + (j + 1) * P]
                nc.tensor.matmul(p_z, hA[:, part], t.Wn2a[:], start=True, stop=False)
                nc.tensor.matmul(p_z, hB[:, part], t.Wn2b[:], start=False, stop=True)
                nc.tensor.matmul(p_own, hA[:, part], t.Ws2a[:], start=True, stop=False)
                nc.tensor.matmul(p_own, hB[:, part], t.Ws2b[:], start=False, stop=False)
                nc.tensor.matmul(p_own, xT[:, part], t.identity[:], start=False, stop=False)
                last = nc.tensor.matmul(p_own, t.ones_row[:], t.b2[0:1, :], start=False, stop=True)
            last.then_inc(out_summed, 1)

    def scalar(act, k, q):
        if q == 2:
            act.wait_ge(flipped, k + 1)
            wait_for(act, out_summed, k)
            nc.scalar.copy(xT[:], p_x[:, 0:PIECE]).then_inc(copied, 1)
        if q == 4:
            act.wait_ge(h_summed, k + 1)
            nc.scalar.activation(hA[:], p_hA, ACT.Relu, bias=t.b1a[:, 0:1])
            nc.scalar.activation(hB[:], p_hB, ACT.Relu, bias=t.b1b[:, 0:1]).then_inc(h_ready, 1)
        if q == 7:
            act.wait_ge(out_summed, k + 1)
            wait_for(act, stored, k * 32)
            nc.scalar.copy(z[:].rearrange("p j f -> p (j f)"), p_out[:, 0:PIECE])
            nc.scalar.copy(own[:].rearrange("p j f -> p (j f)"), p_out[:, PIECE:2 * PIECE]).then_inc(out_ready, 1)

    def vector(dve, k, q, starts):
        if q == 2:
            take_mean(nc, dve, m, t, k, starts, inv, mean, chain, h_summed).then_inc(mean_ready, 1)
            dve.wait_ge(mean_ready, k + 1)

    side = Names()
    side.load, side.store, side.tensor, side.scalar, side.vector = load, store, tensor, scalar, vector
    side.stored, side.count = stored, 32
    side.sems = [x_in, flipped, copied, chain, mean_ready, h_summed, h_ready, out_summed, out_ready, storing, stored]
    return side


def second_nodes(nc, m, d, t, sb, pb, sem):
    own, u, normed = (sb(n, [P, PARTS, P], FP32) for n in ("piece_own", "piece_u", "piece_normed"))
    inv, mean = sb("piece_inv", [P, PIECE], FP32), sb("piece_mean", [P, PIECE], FP32)
    stats, moments = sb("piece_stats", [P, PARTS, 6], FP32), sb("piece_moments", [P, PARTS, 2], FP32)
    std, scale = sb("piece_std", [P, PARTS], FP32), sb("piece_scale", [P, PARTS], FP32)
    x1T = sb("piece_x1T", [P, PIECE], FP32)
    rest, y = sb("piece_rest", [P, PARTS, P], FP32), sb("piece_y", [P, PARTS, P], FP32)
    degrees = sb("piece_degrees", [1, PIECE], FP32)
    p_mean, p_x1, p_y, p_bias = (pb(n, [P, 512], FP32) for n in ("piece_p_mean", "piece_p_x1", "piece_p_y", "piece_p_bias"))
    own_in, chain, mean_ready, mean_flipped = sem("own_in"), sem("inv_chain"), sem("mean_ready"), sem("mean_flipped")
    u_ready, stats_ready, aggregate_started = sem("u_ready"), sem("stats_ready"), sem("aggregate_started")
    moments_ready, std_ready, scale_ready = sem("moments_ready"), sem("std_ready"), sem("scale_ready")
    normed_ready, bias_summed, rest_ready = sem("normed_ready"), sem("bias_summed"), sem("rest_ready")
    x1_flipped, x1_copied, y_summed, y_ready = sem("x1_flipped"), sem("x1_copied"), sem("y_summed"), sem("y_ready")
    storing, stored = sem("storing"), sem("stored")

    def load(sp, k, starts):
        wait_for(sp, u_ready, k)
        sp.dma_start(own[:], piece_rows(d["own"], piece_start(sp, m, starts, k))).then_inc(own_in, 16)

    def store(sp, k, starts):
        sp.wait_ge(y_ready, k + 1)
        sp.wait_ge(rest_ready, k + 1)
        sp.sem_inc(storing, 1)
        first = piece_start(sp, m, starts, k)
        sp.dma_start(piece_rows(d["rest"], first), rest[:]).then_inc(stored, 16)
        sp.dma_start(piece_rows(d["y"], first), y[:]).then_inc(stored, 16)

    def tensor(pe, k, q):
        if q == 3:
            pe.wait_ge(mean_ready, k + 1)
            wait_for(pe, u_ready, k)
            for j in range(PARTS):
                last = nc.tensor.transpose(p_mean[:, j * P:(j + 1) * P], mean[:, j * P:(j + 1) * P], t.identity[:])
            last.then_inc(mean_flipped, 1)
        if q == 4:
            wait_for(pe, rest_ready, k)
            for j in range(PARTS):
                part = slice(j * P, (j + 1) * P)
                last = nc.tensor.matmul(p_bias[:, part], degrees[:, part], t.bm2[0:1, :], start=True, stop=True)
            last.then_inc(bias_summed, 1)
        if q == 6:
            pe.wait_ge(normed_ready, k + 1)
            wait_for(pe, x1_copied, k)
            for j in range(PARTS):
                last = nc.tensor.transpose(p_x1[:, j * P:(j + 1) * P], normed[:, j, :], t.identity[:])
            last.then_inc(x1_flipped, 1)
        if q == 8:
            pe.wait_ge(x1_copied, k + 1)
            wait_for(pe, y_ready, k)
            for j in range(PARTS):
                part = slice(j * P, (j + 1) * P)
                nc.tensor.matmul(p_y[:, part], x1T[:, part], t.Wm_x[:], start=True, stop=False)
                last = nc.tensor.matmul(p_y[:, part], t.ones_row[:], t.bm1[0:1, :], start=False, stop=True)
            last.then_inc(y_summed, 1)

    def scalar(act, k, q):
        if q == 4:
            act.wait_ge(moments_ready, k + 1)
            nc.scalar.activation(std[:], moments[:, :, 1], ACT.Sqrt, bias=t.eps[:, 0:1]).then_inc(std_ready, 1)
        if q == 7:
            act.wait_ge(x1_flipped, k + 1)
            wait_for(act, y_summed, k)
            nc.scalar.copy(x1T[:], p_x1[:, 0:PIECE]).then_inc(x1_copied, 1)
        if q == 9:
            act.wait_ge(y_summed, k + 1)
            wait_for(act, stored, k * 32)
            nc.scalar.copy(y[:].rearrange("p j f -> p (j f)"), p_y[:, 0:PIECE]).then_inc(y_ready, 1)

    def vector(dve, k, q, starts):
        if q == 2:
            wait_for(dve, bias_summed, k)
            nc.vector.tensor_copy(degrees[:], t.degree[0:1, ds(piece_start(dve, m, starts, k), PIECE)])
            take_mean(nc, dve, m, t, k, starts, inv, mean, chain, mean_flipped).then_inc(mean_ready, 1)
            dve.wait_ge(mean_ready, k + 1)
        if q == 5:
            dve.wait_ge(own_in, k * 16 + 16)
            dve.wait_ge(mean_flipped, k + 1)
            wait_for(dve, normed_ready, k)
            nc.vector.tensor_tensor(u[:].rearrange("p j f -> p (j f)"), p_mean[:, 0:PIECE],
                                    own[:].rearrange("p j f -> p (j f)"), ALU.add).then_inc(u_ready, 1)
            dve.wait_ge(u_ready, k + 1)
            for j in range(PARTS):
                last = nc.vector.bn_stats(stats[:, j, :], u[:, j, :])
            last.then_inc(stats_ready, 1)
            dve.wait_ge(stats_ready, k + 1)
            dve.sem_inc(aggregate_started, 1)
            for j in range(PARTS):
                last = nc.vector.bn_aggr(moments[:, j, :], stats[:, j, :])
            last.then_inc(moments_ready, 1)
        if q == 6:
            dve.wait_ge(std_ready, k + 1)
            nc.vector.reciprocal(scale[:], std[:]).then_inc(scale_ready, 1)
            dve.wait_ge(scale_ready, k + 1)
            wait_for(dve, rest_ready, k)
            wait_for(dve, x1_flipped, k)
            for j in range(PARTS):
                last = nc.vector.tensor_scalar(normed[:, j, :], u[:, j, :], moments[:, j, 0:1], scale[:, j:j + 1],
                                               ALU.subtract, ALU.mult)
            last.then_inc(normed_ready, 1)
        if q == 7:
            dve.wait_ge(normed_ready, k + 1)
            dve.wait_ge(bias_summed, k + 1)
            wait_for(dve, stored, k * 32)
            nc.vector.scalar_tensor_tensor(rest[:].rearrange("p j f -> p (j f)"), normed[:].rearrange("p j f -> p (j f)"),
                                           2.0, p_bias[:, 0:PIECE], ALU.mult, ALU.add).then_inc(rest_ready, 1)

    side = Names()
    side.load, side.store, side.tensor, side.scalar, side.vector = load, store, tensor, scalar, vector
    side.stored, side.count = stored, 32
    side.sems = [own_in, chain, mean_ready, mean_flipped, u_ready, stats_ready, aggregate_started, moments_ready, std_ready,
                 scale_ready, normed_ready, bias_summed, rest_ready, x1_flipped, x1_copied, y_summed, y_ready, storing, stored]
    return side


def sum_neighbours(nc, m, d, t, table, count_degrees, nodes_step, sb, pb, sem):
    side = nodes_step(nc, m, d, t, sb, pb, sem)
    idx = sb("idx", [P, UNROLL, TILES], I32)
    rows = sb("rows", [P, UNROLL, TILES, P], FP32)
    hot = sb("hot", [P, UNROLL, TILES, WIN], FP32)
    bank = (0, 1, 0, 1, 2)
    win = [pb(f"win{b}", [P, 512], FP32) for b in range(3)]
    idx_loaded, gathers_started = sem("idx_loaded"), sem("gathers_started")
    rows_arrived = [[sem(f"rows_arrived{q}_{j}") for j in range(TILES)] for q in range(UNROLL)]
    hot_ready, sums_ready, window_added = sem("hot_ready"), sem("sums_ready"), sem("window_added")
    chain, base_ready = sem("chain"), sem("base_ready")
    sems = [idx_loaded, gathers_started, *[a for slot in rows_arrived for a in slot], hot_ready, sums_ready, window_added, chain, base_ready, *side.sems]

    def one_pass():
        with nc.Block() as block:
            @block.gpsimd
            def _(pool):
                gather_groups(nc, pool, m, table, idx, rows, idx_loaded, sums_ready, gathers_started, rows_arrived)

            @block.scalar
            def _(act):
                def step(i, q):
                    now = item(i, q, 0, UNROLL, m.NG)
                    if now:
                        g, _, slot = now
                        wait_for(act, sums_ready, g - UNROLL + 1)
                        nc.scalar.copy(idx[:, slot, :], t.src_idx[:, ds(g, 1), :].rearrange("p o j -> p (o j)")
                                       ).then_inc(idx_loaded, 1)
                    piece_steps(side.scalar, act, m, i - 1, q)
                edge_sweep(act, step, m.NG, UNROLL, 3 * UNROLL, 4)

            @block.vector
            def _(dve):
                set_windows(nc, dve, m, t, chain, base_ready)

                def step(i, q):
                    now = item(i, q, 0, UNROLL, m.NG)
                    if now:
                        g, _, slot = now
                        wait_for(dve, sums_ready, g - UNROLL + 1)
                        one_hot(nc, t, hot, g, slot).then_inc(hot_ready, 1)
                    late = item(i, q, 2, UNROLL, m.NG)
                    if late:
                        g, _, slot = late
                        base = dve.value_load(t.base_int[0:1, ds(g, 1)], min_val=0, max_val=m.N)
                        wait_for(dve, window_added, g)
                        dve.wait_ge(sums_ready, g + 1)
                        w = ds(base, WIN)
                        if count_degrees:
                            nc.vector.tensor_tensor(t.degree[:, w], t.degree[:, w], win[bank[slot]][:, WIN:2 * WIN], ALU.add)
                        nc.vector.tensor_tensor(t.sums[:, w], t.sums[:, w], win[bank[slot]][:, 0:WIN],
                                                ALU.add).then_inc(window_added, 1)
                    if q == 2:
                        dve.wait_ge(window_added, min(i * UNROLL + 1, m.NG) if isinstance(i, int) else i * UNROLL + 1)
                    piece_steps(lambda dve, k, s: side.vector(dve, k, s, t.piece_start), dve, m, i, q)
                edge_sweep(dve, step, m.NG, UNROLL, 2 * UNROLL, 3)

            @block.tensor
            def _(pe):
                def step(i, q):
                    now = item(i, q, 0, UNROLL, m.NG)
                    if now:
                        g = now[0]
                        wait_for(pe, window_added, g - 1)
                        pe.wait_ge(hot_ready, g + 1)
                        for j in range(TILES):
                            pe.wait_ge(rows_arrived[q][j], i * 16 + 16)
                        for j in range(TILES):
                            last = nc.tensor.matmul(win[bank[q]][:, 0:WIN], rows[:, q, j, :], hot[:, q, j, :],
                                                    start=j == 0, stop=j == TILES - 1)
                        if count_degrees:
                            for j in range(TILES):
                                last = nc.tensor.matmul(win[bank[q]][:, WIN:2 * WIN], t.ones[:], hot[:, q, j, :],
                                                        start=j == 0, stop=j == TILES - 1)
                        last.then_inc(sums_ready, 1)
                    piece_steps(side.tensor, pe, m, i, q)
                edge_sweep(pe, step, m.NG, UNROLL, 2 * UNROLL, 3)

            @block.sync
            def _(sp):
                side.load(sp, 0, t.piece_start)
                side.load(sp, 1, t.piece_start)
                side.store(sp, 0, t.piece_start)
                with sp.Fori(2, m.PIECES) as k:
                    side.load(sp, k, t.piece_start)
                    side.store(sp, k - 1, t.piece_start)
                side.store(sp, m.PIECES - 1, t.piece_start)
                sp.wait_ge(side.stored, side.count * m.PIECES)
        clear_counts(nc, sems, gathered=True)

    all_passes(nc, m, t, one_pass)
    again = nc.values_load(t.again[0:1, 0:1], min_val=0, max_val=1)
    with nc.If(again > 0):
        pieces_alone(nc, m, t, side)


def all_passes(nc, m, t, one_pass):
    passes = nc.values_load(t.passes[0:1, 0:1], min_val=1, max_val=m.WINDOWS)
    fine = -(-round(m.WINDOWS ** (1 / 3) * 100) // 100)
    with nc.Fori(0, m.WINDOWS, fine * fine) as outer:
        with nc.If(outer < passes):
            with nc.Fori(0, fine * fine, fine) as middle:
                with nc.If(outer + middle < passes):
                    with nc.Fori(0, fine) as inner:
                        with nc.If(outer + middle + inner < passes):
                            one_pass()


def clear_sums(nc, m, t, tiles, sb, pb, sem):
    width = m.N + WIN
    cuts = [0, width // 3, 2 * width // 3, width]
    with nc.Block() as block:
        @block.vector
        def _(dve):
            nc.vector.memset(t.slow_base[:], 0.0)
            for tile in tiles:
                nc.vector.memset(tile[:, cuts[0]:cuts[1]], 0.0)

        @block.gpsimd
        def _(pool):
            for tile in tiles:
                nc.gpsimd.memset(tile[:, cuts[1]:cuts[2]], 0.0)

        @block.scalar
        def _(act):
            for tile in tiles:
                nc.scalar.copy(tile[:, cuts[2]:cuts[3]], t.zeros[:].to_broadcast([P, cuts[3] - cuts[2]]))


def by_sub(ap):
    return ap.rearrange("f (p j) -> f j p", j=NJ)


def node_rows(ap, n):
    return ap.rearrange("(b p j) f -> b p (j f)", p=SUB, j=NJ)[ds(n, 1), :, :].rearrange("o p c -> (o p) c")


def third_nodes(nc, m, d, t, sb, pb, sem):
    rest, u, normed = (sb(n, [SUB, 2, NJ, P], FP32) for n in ("rest", "u", "normed"))
    stats, moments = sb("stats", [SUB, 2, NJ, 6], FP32), sb("moments", [SUB, 2, NJ, 2], FP32)
    std, scale, shift = (sb(n, [SUB, 2, NJ], FP32) for n in ("std", "scale", "shift"))
    total = sb("total", [P, 2, BLOCK], FP32)
    p_out = [pb("p_out0", [P, 512], FP32), pb("p_out1", [P, 512], FP32)]
    rest_in, stored = [sem("rest_in0"), sem("rest_in1")], [sem("stored0"), sem("stored1")]
    total_ready, out_summed = sem("total_ready"), sem("out_summed")
    u_ready, stats_ready, aggregates_started = sem("u_ready"), sem("stats_ready"), sem("aggregates_started")
    moments_ready, std_ready = sem("moments_ready"), sem("std_ready")
    scale_ready, shift_ready = sem("scale_ready"), sem("shift_ready")
    first_normed, last_normed = sem("first_normed"), sem("last_normed")
    HALF = NJ // 2

    def flat(ap):
        return ap.rearrange("p j f -> p (j f)")

    with nc.Block() as block:
        @block.sync
        def _(sp):
            def step(n, slot, turn):
                now = block_before(n, slot, turn, 0, m.NB)
                if now:
                    wait_for(sp, u_ready, n - 1)
                    copy_rows(sp, flat(rest[:, slot]), node_rows(d["rest"], n), rest_in[slot])
                late = block_before(n, slot, turn, 3, m.NB)
                if late:
                    b, s, _ = late
                    sp.wait_ge(first_normed, b + 1)
                    sp.wait_ge(last_normed, b + 1)
                    copy_rows(sp, node_rows(d["out"], b), flat(normed[:, s]), stored[s])
            node_sweep(sp, step, m.NB, 3)
            for slot in range(2):
                sp.wait_ge(stored[slot], 32 * ((m.NB + 1 - slot) // 2))

        @block.scalar
        def _(act):
            def step(n, slot, turn):
                now = block_before(n, slot, turn, 0, m.NB)
                if now:
                    wait_for(act, out_summed, n - 1)
                    nc.scalar.copy(total[:, slot], t.sums[:, ds(n * BLOCK, BLOCK)]).then_inc(total_ready, 1)
                late = block_before(n, slot, turn, 2, m.NB)
                if late:
                    b, s, use = late
                    act.wait_ge(moments_ready, b + 1)
                    nc.scalar.activation(std[:, s, :], moments[:, s, :, 1], ACT.Sqrt, bias=t.eps[0:SUB, 0:1]
                                         ).then_inc(std_ready, 1)
                    act.wait_ge(shift_ready, b + 1)
                    wait_for(act, stored[s], use * 32)
                    for j in range(HALF, NJ):
                        ins = nc.scalar.activation(normed[:, s, j, :], u[:, s, j, :], ACT.Identity,
                                                   bias=shift[:, s, j:j + 1], scale=scale[:, s, j:j + 1])
                    ins.then_inc(last_normed, 1)
            node_sweep(act, step, m.NB, 2)

        @block.tensor
        def _(pe):
            def step(n, slot, turn):
                pe.wait_ge(total_ready, n + 1)
                wait_for(pe, u_ready, n - 1)
                for j in range(NJ):
                    last = nc.tensor.matmul(p_out[slot][0:SUB, j * P:(j + 1) * P], by_sub(total[:, slot])[:, j, :],
                                            t.Wm2[:], start=True, stop=True)
                last.then_inc(out_summed, 1)
            node_sweep(pe, step, m.NB)

        @block.vector
        def _(dve):
            def step(n, slot, turn):
                now = block_before(n, slot, turn, 0, m.NB)
                if now:
                    b, s, use = now
                    dve.wait_ge(out_summed, b + 1)
                    dve.wait_ge(rest_in[s], use * 32 + 32)
                    wait_for(dve, first_normed, b - 1)
                    wait_for(dve, last_normed, b - 1)
                    nc.vector.tensor_tensor(flat(u[:, s]), p_out[s][0:SUB, :], flat(rest[:, s]), ALU.add
                                            ).then_inc(u_ready, 1)
                late = block_before(n, slot, turn, 1, m.NB)
                if late:
                    b, s, use = late
                    dve.wait_ge(std_ready, b + 1)
                    nc.vector.reciprocal(scale[:, s, :], std[:, s, :]).then_inc(scale_ready, 1)
                    dve.wait_ge(scale_ready, b + 1)
                    wait_for(dve, stored[s], use * 32)
                    nc.vector.scalar_tensor_tensor(shift[:, s, :], moments[:, s, :, 0], -1.0, scale[:, s, :],
                                                   ALU.mult, ALU.mult).then_inc(shift_ready, 1)
                    for j in range(HALF):
                        last = nc.vector.tensor_scalar(normed[:, s, j, :], u[:, s, j, :], moments[:, s, j, 0:1],
                                                       scale[:, s, j:j + 1], ALU.subtract, ALU.mult)
                    last.then_inc(first_normed, 1)
                if now:
                    b, s, use = now
                    dve.wait_ge(u_ready, b + 1)
                    for j in range(NJ):
                        last = nc.vector.bn_stats(stats[:, s, j, :], u[:, s, j, :])
                    last.then_inc(stats_ready, 1)
                    dve.wait_ge(stats_ready, b + 1)
                    dve.sem_inc(aggregates_started, 1)
                    for j in range(NJ):
                        last = nc.vector.bn_aggr(moments[:, s, j, :], stats[:, s, j, :])
                    last.then_inc(moments_ready, 1)
            node_sweep(dve, step, m.NB, 1)


def sum_messages(nc, m, d, t, sb, pb, sem):
    A = d["attr"].shape[1]
    idx = sb("idx", [P, UNROLL, TILES], I32)
    rows = sb("rows", [P, UNROLL, TILES, P], FP32)
    hot = sb("hot", [P, UNROLL, TILES, WIN], FP32)
    attr = sb("attr", [P, UNROLL, TILES, A], FP32)
    when = sb("when", [9, UNROLL, GROUP], BF16)
    wide = 3 * P
    attrT = sb("attrT", [A, 2, wide], FP32)
    hid = sb("hid", [P, 2, wide], FP32)
    gate = sb("gate", [P, 2, wide], FP32)
    gated = sb("gated", [P, 2, wide], FP32)
    p_attr, p_hid, p_edge = pb("p_attr", [P, 512], FP32), pb("p_hid", [P, 512], FP32), pb("p_edge", [P, 512], FP32)
    p_time, p_msg = pb("p_time", [P, 512], FP32), pb("p_msg", [P, 512], FP32)
    win = [pb("win0", [P, 512], FP32), pb("win1", [P, 512], FP32)]
    idx_loaded, gathers_started = sem("idx_loaded"), sem("gathers_started")
    rows_arrived = [[sem(f"rows_arrived{q}_{j}") for j in range(TILES)] for q in range(UNROLL)]
    attr_arrived = [sem(f"attr_arrived{q}") for q in range(UNROLL)]
    when_arrived = [sem(f"when_arrived{q}") for q in range(UNROLL)]
    hot_ready, sums_ready, window_added = sem("hot_ready"), sem("sums_ready"), sem("window_added")
    chain, base_ready = sem("chain"), sem("base_ready")
    attr_flipped, attr_copied = sem("attr_flipped"), sem("attr_copied")
    hid_summed, hid_ready = sem("hid_summed"), sem("hid_ready")
    edge_summed, time_summed, gate_ready, gated_ready = sem("edge_summed"), sem("time_summed"), sem("gate_ready"), sem("gated_ready")
    msg_summed, msg_added, msg_ready = sem("msg_summed"), sem("msg_added"), sem("msg_ready")
    sems = [idx_loaded, gathers_started, *[a for slot in rows_arrived for a in slot], *attr_arrived, *when_arrived, hot_ready, sums_ready,
            window_added, chain, base_ready, attr_flipped, attr_copied, hid_summed, hid_ready, edge_summed,
            time_summed, gate_ready, gated_ready, msg_summed, msg_added, msg_ready]
    NC = 2 * m.NG
    attr_d = d["attr"].rearrange("(g p j) a -> g p (j a)", p=P, j=TILES)

    def chunk(i, q, lag):
        found = item(i, q, lag, CHUNKS, NC)
        if found is None:
            return None
        c, body, at = found
        k = Names()
        k.c, k.buf, k.first = c, at % 2, at % 2 == 0
        k.group, k.body, k.slot = body * UNROLL + at // 2, body, at // 2
        k.t0, k.t1 = CHUNK_TILES[at % 2]
        k.nt = k.t1 - k.t0
        k.w = k.nt * P
        return k

    def one_pass():
        with nc.Block() as block:
            @block.gpsimd
            def _(pool):
                gather_groups(nc, pool, m, d["y"], idx, rows, idx_loaded, sums_ready, gathers_started, rows_arrived)

            @block.sync
            def _(sp):
                def step(i, q):
                    g = i * UNROLL + q
                    wait_for(sp, attr_flipped, g * 2 - 2 * UNROLL + 2)
                    sp.dma_start(attr[:, q].rearrange("p j a -> p (j a)"),
                                 attr_d[ds(g, 1), :, :].rearrange("o p c -> (o p) c")).then_inc(attr_arrived[q], 16)
                    wait_for(sp, time_summed, g * 2 - 2 * UNROLL + 2)
                    for c in range(3):
                        sp.dma_start(when[3 * c:3 * c + 3, q, :],
                                     d["weight_parts"][c:c + 1, ds(g * GROUP, GROUP)].to_broadcast([3, GROUP])
                                     ).then_inc(when_arrived[q], 16)
                edge_sweep(sp, step, m.NG, UNROLL, 0)

            @block.tensor
            def _(pe):
                def step(i, q):
                    k = chunk(i, q, 0)
                    if k:
                        pe.wait_ge(attr_arrived[k.slot], k.body * 16 + 16)
                        wait_for(pe, attr_copied, k.c)
                    k = chunk(i, q, 1)
                    if k:
                        pe.wait_ge(attr_copied, k.c + 1)
                        wait_for(pe, hid_ready, k.c)
                        nc.tensor.matmul(p_hid[:, 0:k.w], t.We1[:], attrT[:, k.buf, 0:k.w], start=True, stop=True
                                         ).then_inc(hid_summed, 1)
                    k = chunk(i, q, 0)
                    if k:
                        for j in range(k.t0, k.t1):
                            last = nc.tensor.transpose(p_attr[0:A, (j - k.t0) * P:(j - k.t0 + 1) * P], attr[:, k.slot, j, :],
                                                       t.identity[:])
                        last.then_inc(attr_flipped, 1)
                    k = chunk(i, q, 2)
                    if k:
                        pe.wait_ge(when_arrived[k.slot], k.body * 48 + 48)
                        wait_for(pe, gate_ready, k.c)
                        nc.tensor.matmul(p_time[:, 0:k.w].rearrange("f (j p) -> f j p", p=P), t.Wt9[:],
                                         when[:, k.slot, :].rearrange("r (p j) -> r j p", j=TILES)[:, k.t0:k.t1, :],
                                         start=True, stop=True).then_inc(time_summed, 1)
                        pe.wait_ge(hid_ready, k.c + 1)
                        wait_for(pe, gated_ready, k.c)
                        nc.tensor.matmul(p_edge[:, 0:k.w], t.We2[:], hid[:, k.buf, 0:k.w], start=True, stop=True
                                         ).then_inc(edge_summed, 1)
                    k = chunk(i, q, 3)
                    if k:
                        pe.wait_ge(gated_ready, k.c + 1)
                        wait_for(pe, msg_added, k.c)
                        for j in range(k.nt):
                            last = nc.tensor.matmul(p_msg[:, j * P:(j + 1) * P], gated[:, k.buf, j * P:(j + 1) * P], t.Wm_e[:],
                                                    start=True, stop=True)
                        last.then_inc(msg_summed, 1)
                    k = chunk(i, q, 6)
                    if k and k.first:
                        pe.wait_ge(msg_ready, k.c + 2)
                        pe.wait_ge(hot_ready, k.group + 1)
                        wait_for(pe, window_added, k.group if k.slot == 0 else k.group - 1)
                        for j in range(TILES):
                            last = nc.tensor.matmul(win[k.slot % 2][:, 0:WIN], rows[:, k.slot, j, :], hot[:, k.slot, j, :],
                                                    start=j == 0, stop=j == TILES - 1)
                        last.then_inc(sums_ready, 1)
                edge_sweep(pe, step, NC, CHUNKS, 7)

            @block.scalar
            def _(act):
                def step(i, q):
                    k = chunk(i, q, 0)
                    if k and k.first:
                        wait_for(act, msg_added, k.c - 2 * UNROLL + 2)
                        nc.scalar.copy(idx[:, k.slot, :], t.src_idx[:, ds(k.group, 1), :].rearrange("p o j -> p (o j)")
                                       ).then_inc(idx_loaded, 1)
                    if k:
                        act.wait_ge(attr_flipped, k.c + 1)
                        wait_for(act, hid_summed, k.c - 1)
                        nc.scalar.copy(attrT[:, k.buf, 0:k.w], p_attr[0:A, 0:k.w]).then_inc(attr_copied, 1)
                    k = chunk(i, q, 1)
                    if k:
                        act.wait_ge(hid_summed, k.c + 1)
                        wait_for(act, edge_summed, k.c - 1)
                        nc.scalar.activation(hid[:, k.buf, 0:k.w], p_hid[:, 0:k.w], ACT.Relu, bias=t.be1[:, 0:1]
                                             ).then_inc(hid_ready, 1)
                    k = chunk(i, q, 2)
                    if k:
                        act.wait_ge(time_summed, k.c + 1)
                        wait_for(act, gated_ready, k.c - 1)
                        nc.scalar.activation(gate[:, k.buf, 0:k.w], p_time[:, 0:k.w], ACT.Sigmoid, bias=t.bt[:, 0:1]
                                             ).then_inc(gate_ready, 1)
                    k = chunk(i, q, 4)
                    if k:
                        act.wait_ge(msg_added, k.c + 1)
                        nc.scalar.activation(rows[:, k.slot, k.t0:k.t1, :], rows[:, k.slot, k.t0:k.t1, :], ACT.Relu
                                             ).then_inc(msg_ready, 1)
                edge_sweep(act, step, NC, CHUNKS, 4)

            @block.vector
            def _(dve):
                set_windows(nc, dve, m, t, chain, base_ready)

                def step(i, q):
                    k = chunk(i, q, 2)
                    if k:
                        dve.wait_ge(gate_ready, k.c + 1)
                        dve.wait_ge(edge_summed, k.c + 1)
                        wait_for(dve, msg_summed, k.c - 1)
                        nc.vector.scalar_tensor_tensor(gated[:, k.buf, 0:k.w], p_edge[:, 0:k.w], t.be2[:, 0:1],
                                                       gate[:, k.buf, 0:k.w], ALU.add, ALU.mult).then_inc(gated_ready, 1)
                    k = chunk(i, q, 3)
                    if k:
                        for j in range(k.t0, k.t1):
                            dve.wait_ge(rows_arrived[k.slot][j], k.body * 16 + 16)
                        dve.wait_ge(msg_summed, k.c + 1)
                        at = rows[:, k.slot, k.t0:k.t1, :].rearrange("p j f -> p (j f)")
                        nc.vector.tensor_tensor(at, p_msg[:, 0:k.w], at, ALU.add).then_inc(msg_added, 1)
                    k = chunk(i, q, 4)
                    if k and k.first:
                        wait_for(dve, sums_ready, k.group - UNROLL + 1)
                        one_hot(nc, t, hot, k.group, k.slot).then_inc(hot_ready, 1)
                    k = chunk(i, q, 7)
                    if k and k.first:
                        base = dve.value_load(t.base_int[0:1, ds(k.group, 1)], min_val=0, max_val=m.N)
                        wait_for(dve, window_added, k.group)
                        dve.wait_ge(sums_ready, k.group + 1)
                        w = ds(base, WIN)
                        nc.vector.tensor_tensor(t.sums[:, w], t.sums[:, w], win[k.slot % 2][:, 0:WIN],
                                                ALU.add).then_inc(window_added, 1)
                edge_sweep(dve, step, NC, CHUNKS, 8)
        clear_counts(nc, sems, gathered=True)

    all_passes(nc, m, t, one_pass)


def gnn(nc, d):
    m = Names()
    m.N, F = d["x"].shape
    m.E = d["src"].shape[0]
    m.H = d["Ws1"].shape[1]
    m.NG = m.E // GROUP
    m.NB = m.N // BLOCK
    assert F == P and m.NG * GROUP == m.E and m.NG % UNROLL == 0 and m.NB * BLOCK == m.N and m.E % (SUB * GROUP) == 0
    m.PIECES = m.NG // UNROLL
    assert m.PIECES * PIECE >= m.N
    m.WINDOWS = -(-m.N // WIN)
    d["low"], d["span"] = (nc.dram_tensor(n, [m.NG], FP32).ap() for n in ("group_low", "group_span"))
    d["weight_parts"] = nc.dram_tensor("weight_parts", [3, m.E], BF16).ap()
    d["wt_parts"] = nc.dram_tensor("wt_parts_d", [3, P], BF16).ap()
    d["z"], d["own"], d["rest"], d["y"] = (nc.dram_tensor(n, [m.N, P], FP32).ap() for n in ("z_d", "own_d", "rest_d", "y_d"))

    with ExitStack() as whole:
        def run(tag, build, *args):
            with ExitStack() as part:
                sems = []

                def sem(name):
                    sems.append(part.enter_context(nc.semaphore(tag + name)))
                    return sems[-1]

                build(*args, lambda n, s, dt: part.enter_context(nc.sbuf_tensor(tag + n, s, dt)),
                      lambda n, s, dt: part.enter_context(nc.psum_tensor(tag + n, s, dt)), sem)
                clear_counts(nc, sems)

        def sb(name, shape, dt):
            return whole.enter_context(nc.sbuf_tensor(name, shape, dt))

        t = Names()
        t.rel = sb("rel", [P, m.NG, TILES], FP32)
        t.src_idx = sb("src_idx", [P, m.NG, TILES], I32)
        t.fast_base, t.base_now, t.base_next = (sb(n, [P, m.NG], FP32) for n in ("fast_base", "base_now", "base_next"))
        t.base_int = sb("base_int", [1, m.NG], I32)
        t.piece_start, t.every_start = sb("piece_start", [1, m.PIECES], I32), sb("every_start", [1, m.PIECES], I32)
        t.passes, t.again = sb("passes", [1, 1], I32), sb("again", [1, 1], I32)
        t.slow_base, t.window_step = sb("slow_base", [P, 1], FP32), sb("window_step", [P, 1], FP32)
        t.identity = sb("identity", [P, P], FP32)
        t.ones, t.ones_row, t.eps = sb("ones", [P, P], FP32), sb("ones_row", [1, P], FP32), sb("eps", [P, 1], FP32)
        t.We1 = sb("We1", list(d["We1"].shape), FP32)
        t.We2, t.Wm_x, t.Wm_e, t.Wm2 = (sb(n, [P, P], FP32) for n in ("We2", "Wm_x", "Wm_e", "Wm2"))
        t.Ws1, t.Wn1 = sb("Ws1", [P, m.H], FP32), sb("Wn1", [P, m.H], FP32)
        t.Wn2a, t.Ws2a = sb("Wn2a", [P, P], FP32), sb("Ws2a", [P, P], FP32)
        t.Wn2b, t.Ws2b = sb("Wn2b", [m.H - P, P], FP32), sb("Ws2b", [m.H - P, P], FP32)
        t.b1a, t.b1b = sb("b1a", [P, 1], FP32), sb("b1b", [m.H - P, 1], FP32)
        t.be1, t.be2, t.bt = (sb(n, [P, 1], FP32) for n in ("be1", "be2", "bt"))
        t.b2, t.bm1, t.bm2 = (sb(n, [P, P], FP32) for n in ("b2", "bm1", "bm2"))
        t.Wt9 = sb("Wt9", [9, P], BF16)
        t.iota_ps = whole.enter_context(nc.psum_tensor("iota_ps", [P, 512], FP32))

        t.zeros = sb("zeros", [P, 1], FP32)
        t.sums = sb("sums", [P, m.N + WIN], FP32)
        run("load_", load_and_index, nc, m, d, t)
        with nc.sbuf_tensor("degree", [P, m.N + WIN], FP32) as t.degree:
            run("clear_x_", clear_sums, nc, m, t, [t.degree])
            run("sum_x_", sum_neighbours, nc, m, d, t, d["x"], True, first_nodes)
            run("clear_z_", clear_sums, nc, m, t, [t.sums])
            run("sum_z_", sum_neighbours, nc, m, d, t, d["z"], False, second_nodes)
            run("clear_y_", clear_sums, nc, m, t, [t.sums])
        run("messages_", sum_messages, nc, m, d, t)
        run("third_", third_nodes, nc, m, d, t)


INPUTS = {
    "x": "x", "src": "src", "dst": "dst", "edge_attr_64": "attr", "edge_weight": "edge_weight",
    "L0_gnn_W_self1": "Ws1", "L0_gnn_W_neigh1": "Wn1", "L0_gnn_b1": "b1",
    "L0_gnn_W_self2": "Ws2", "L0_gnn_W_neigh2": "Wn2", "L0_gnn_b2": "b2",
    "L1_gnn_We1": "We1", "L1_gnn_be1": "be1", "L1_gnn_We2": "We2", "L1_gnn_be2": "be2",
    "L1_gnn_Wt": "Wt", "L1_gnn_bt": "bt", "L1_gnn_Wn1": "Wm1", "L1_gnn_bn1": "bm1",
    "L1_gnn_Wn2": "Wm2", "L1_gnn_bn2": "bm2",
}


def kernel(**inputs):
    import numpy as np
    import concourse.bacc as bacc
    from concourse.bass_utils import run_bass_kernel_spmd

    nc = bacc.Bacc("TRN2", target_bir_lowering=False, num_devices=1)
    arrays, d = {}, {}
    for name, short in INPUTS.items():
        a = np.ascontiguousarray(inputs[name])
        arrays[f"in_{name}"] = a
        ap = nc.dram_tensor(f"in_{name}", a.shape, mybir.dt.from_np(a.dtype), kind="ExternalInput").ap()
        d[short] = ap
    d["out"] = nc.dram_tensor("out", list(inputs["x"].shape), FP32, kind="ExternalOutput").ap()
    gnn(nc, d)
    got = run_bass_kernel_spmd(nc, [arrays], core_ids=[0])
    return got.results[0]["out"]
```
